# Optimizing a Trainium2 kernel written in Bass

```python
import numpy as np
import jax
import jax.numpy as jnp

def _softmax(x, axis=-1):
    return jax.nn.softmax(x, axis=axis)

def _gelu(x):
    return jax.nn.gelu(x, approximate=True)

def _silu(x):
    return jax.nn.silu(x)

def _sigmoid(x):
    return jax.nn.sigmoid(x)

def _layernorm(x, axis=-1, eps=1e-05):
    m = jnp.mean(x, axis=axis, keepdims=True)
    v = jnp.var(x, axis=axis, keepdims=True)
    return (x - m) / jnp.sqrt(v + eps)

def _scatter_add(tgt, idx, src, axis=0):
    return tgt.at[idx].add(src)

def _segment_sum(src, seg, n):
    return jax.ops.segment_sum(src, seg, n)
kernel_name = 'mk_gnn_preln_d1_gnn_r8_4f04fe'

def setup_inputs(seed: int=0):
    np.random.seed(seed)
    _w = jnp.asarray

    def _rec_inputs():
        import jax
        import jax.numpy as jnp
        _gk = jax.random.key(seed)
        x = -0.0005121 + 1.001 * jax.random.normal(jax.random.fold_in(_gk, 1), (12500, 64), jnp.float32)
        src = jax.random.randint(jax.random.fold_in(_gk, 2), (400000,), 0, 12500, jnp.int32)
        dst = jax.random.randint(jax.random.fold_in(_gk, 3), (400000,), 0, 12500, jnp.int32)
        _o = jnp.argsort(dst, stable=True)
        src = src[_o]
        dst = dst[_o]
        edge_attr_64 = 0.000189758 + 1.00013 * jax.random.normal(jax.random.fold_in(_gk, 11), (400000, 64), jnp.float32)
        return (x, src, dst, edge_attr_64)
    x, src, dst, edge_attr_64 = _rec_inputs()

    def _L0_gnn_setup():
        import jax, jax.numpy as jnp
        import numpy as np
        N_NODES = 6250
        N_EDGES = 100000
        NODE_DIM = 64
        EDGE_DIM = 64
        HIDDEN = 128
        FLOW_DIM = 64

        def _mlp2(h, W1, b1, W2, b2):
            return jax.nn.relu(jax.nn.relu(h @ W1 + b1) @ W2 + b2)
        key = jax.random.key(seed)
        ks = jax.random.split(key, 16)
        d_in = NODE_DIM + EDGE_DIM
        s = lambda f: (1.0 / np.sqrt(f)).astype(np.float32)
        inp = {'x': jax.random.normal(ks[0], (N_NODES, NODE_DIM), jnp.float32), 'edge_index': jax.random.randint(ks[1], (2, N_EDGES), 0, N_NODES, jnp.int64), 'edge_attr': jax.random.normal(ks[2], (N_EDGES, EDGE_DIM), jnp.float32), 'Wo1': jax.random.normal(ks[3], (d_in, HIDDEN), jnp.float32) * s(d_in), 'bo1': jnp.zeros((HIDDEN,), jnp.float32), 'Wo2': jax.random.normal(ks[4], (HIDDEN, FLOW_DIM), jnp.float32) * s(HIDDEN), 'bo2': jnp.zeros((FLOW_DIM,), jnp.float32), 'Wi1': jax.random.normal(ks[5], (d_in, HIDDEN), jnp.float32) * s(d_in), 'bi1': jnp.zeros((HIDDEN,), jnp.float32), 'Wi2': jax.random.normal(ks[6], (HIDDEN, FLOW_DIM), jnp.float32) * s(HIDDEN), 'bi2': jnp.zeros((FLOW_DIM,), jnp.float32), 'Wn1': jax.random.normal(ks[7], (2 * FLOW_DIM, HIDDEN), jnp.float32) * s(2 * FLOW_DIM), 'bn1': jnp.zeros((HIDDEN,), jnp.float32), 'Wn2': jax.random.normal(ks[8], (HIDDEN, NODE_DIM), jnp.float32) * s(HIDDEN), 'bn2': jnp.zeros((NODE_DIM,), jnp.float32)}
        return inp
    _L0_gnn_all = _L0_gnn_setup()
    _L0_gnn_in = {k: v for k, v in _L0_gnn_all.items() if k in ('Wo1', 'bo1', 'Wo2', 'bo2', 'Wi1', 'bi1', 'Wi2', 'bi2', 'Wn1', 'bn1', 'Wn2', 'bn2')}
    del _L0_gnn_all
    return {'x': x, 'src': src, 'dst': dst, 'edge_attr_64': edge_attr_64, 'L0_gnn_Wo1': _L0_gnn_in['Wo1'], 'L0_gnn_bo1': _L0_gnn_in['bo1'], 'L0_gnn_Wo2': _L0_gnn_in['Wo2'], 'L0_gnn_bo2': _L0_gnn_in['bo2'], 'L0_gnn_Wi1': _L0_gnn_in['Wi1'], 'L0_gnn_bi1': _L0_gnn_in['bi1'], 'L0_gnn_Wi2': _L0_gnn_in['Wi2'], 'L0_gnn_bi2': _L0_gnn_in['bi2'], 'L0_gnn_Wn1': _L0_gnn_in['Wn1'], 'L0_gnn_bn1': _L0_gnn_in['bn1'], 'L0_gnn_Wn2': _L0_gnn_in['Wn2'], 'L0_gnn_bn2': _L0_gnn_in['bn2']}

def reference(x, src, dst, edge_attr_64, L0_gnn_Wo1, L0_gnn_bo1, L0_gnn_Wo2, L0_gnn_bo2, L0_gnn_Wi1, L0_gnn_bi1, L0_gnn_Wi2, L0_gnn_bi2, L0_gnn_Wn1, L0_gnn_bn1, L0_gnn_Wn2, L0_gnn_bn2):
    import jax
    import jax.numpy as jnp

    def _L0_gnn_ref(x, edge_index, edge_attr, Wo1, bo1, Wo2, bo2, Wi1, bi1, Wi2, bi2, Wn1, bn1, Wn2, bn2):
        import jax, jax.numpy as jnp
        import numpy as np
        N_NODES = 6250
        N_EDGES = 100000
        NODE_DIM = 64
        EDGE_DIM = 64
        HIDDEN = 128
        FLOW_DIM = 64

        def _mlp2(h, W1, b1, W2, b2):
            return jax.nn.relu(jax.nn.relu(h @ W1 + b1) @ W2 + b2)
        n_nodes = x.shape[0]
        row, col = (edge_index[0], edge_index[1])
        edge_in = jnp.concatenate([x[col], edge_attr], axis=1)
        out_mask = (row < col).astype(x.dtype)[:, None]
        in_mask = (row > col).astype(x.dtype)[:, None]
        flow_out = jax.ops.segment_sum(_mlp2(edge_in, Wo1, bo1, Wo2, bo2) * out_mask, row, num_segments=n_nodes)
        flow_in = jax.ops.segment_sum(_mlp2(edge_in, Wi1, bi1, Wi2, bi2) * in_mask, row, num_segments=n_nodes)
        flow = jnp.concatenate([flow_in, flow_out], axis=1)
        return _mlp2(flow, Wn1, bn1, Wn2, bn2)
    edge_index = jnp.stack([src, dst])
    h = jnp.maximum(_layernorm(x, axis=-1), 0.0)
    x = x + _L0_gnn_ref(h, edge_index, edge_attr_64, L0_gnn_Wo1, L0_gnn_bo1, L0_gnn_Wo2, L0_gnn_bo2, L0_gnn_Wi1, L0_gnn_bi1, L0_gnn_Wi2, L0_gnn_bi2, L0_gnn_Wn1, L0_gnn_bn1, L0_gnn_Wn2, L0_gnn_bn2)
    return x

_drawn_inputs = setup_inputs


def setup_inputs(seed=0):
    import zlib

    import numpy as np

    out = dict(_drawn_inputs(seed))
    spreads = {'L0_gnn_bo1': (0.0, 0.1),
     'L0_gnn_bo2': (0.0, 0.1),
     'L0_gnn_bi1': (0.0, 0.1),
     'L0_gnn_bi2': (0.0, 0.1),
     'L0_gnn_bn1': (0.0, 0.641),
     'L0_gnn_bn2': (0.0, 0.51)}
    factors = {}
    for name, (base, spread) in spreads.items():
        noise = np.random.default_rng([zlib.crc32(name.encode()), seed]).standard_normal(out[name].shape)
        drawn = base * np.exp(spread * noise) if base else spread * noise
        out[name] = jnp.asarray(drawn.astype(out[name].dtype))
    for name, factor in factors.items():
        out[name] = (out[name] * factor).astype(out[name].dtype)
    return out
```

```python
from contextlib import ExitStack

import concourse.bass as bass
from concourse import mybir

P = 128
F32 = mybir.dt.float32
BF16 = mybir.dt.bfloat16
I32 = mybir.dt.int32
U32 = mybir.dt.uint32
U16 = mybir.dt.uint16
ALU = mybir.AluOpType
ACT = mybir.ActivationFunctionType
AX_X = mybir.AxisListType.X

FEAT = 64
HID = 128
TILES = 4
GROUP = TILES * P
WINDOW = 64
EPS = 1e-5

C_SLOT = slice(0, TILES)
C_REL = slice(TILES, 2 * TILES)
C_MASKS = slice(2 * TILES, 4 * TILES)
C_IN = slice(2 * TILES, 4 * TILES, 2)
C_OUT = slice(2 * TILES + 1, 4 * TILES, 2)
C_KEY = slice(4 * TILES, 5 * TILES)
FIELDS = 5 * TILES


class Shapes:

    def __init__(self, n_nodes, n_edges):
        self.nodes, self.edges = n_nodes, n_edges
        self.per_part = -(-n_nodes // P)
        self.padded = self.per_part * P
        self.slots = 2 * self.padded
        self.groups = -(-n_edges // GROUP)
        self.last_e0 = n_edges - GROUP
        self.repeated = GROUP * self.groups - n_edges
        self.blocks = -(-self.groups // P)
        assert self.repeated % TILES == 0 and (self.repeated // TILES) % 32 == 0
        assert self.groups >= 16 and n_edges >= GROUP and WINDOW <= self.padded


def gnn_kernel(nc, x, src, dst, ea, Wo1, bo1, Wo2, bo2, Wi1, bi1, Wi2, bi2, Wn1, bn1, Wn2, bn2, out):
    sh = Shapes(x.shape[0], src.shape[0])

    proj = nc.dram_tensor("proj", (sh.padded, 2 * HID), F32, kind="Internal").ap()
    row_keys = nc.dram_tensor("row_keys", (sh.blocks * P, 2 * GROUP), U16, kind="Internal").ap()
    bases = nc.dram_tensor("bases", (sh.blocks, P), I32, kind="Internal").ap()
    tables = [nc.dram_tensor(f"flow{t}", (sh.slots + P, FEAT), F32, kind="Internal").ap() for t in range(TILES)]

    with ExitStack() as ctx:
        def sb(name, shape, dt=F32):
            return ctx.enter_context(nc.sbuf_tensor(name, shape, dt))

        keep = {
            "x_all": sb("x_all", [P, sh.per_part, FEAT]),
            "cols": sb("cols", [P, sh.groups, FIELDS]),
            "ident": sb("ident", [P, P]),
            "tri": sb("tri", [P, P]),
            "pid": sb("pid", [P, 1]),
            "spare": sb("spare", [P, 1]),
            "w_edge": sb("w_edge", [P, HID]),
            "w_second": sb("w_second", [P, 2 * FEAT]),
            "w_n1": sb("w_n1", [P, HID]),
            "w_n2": sb("w_n2", [P, FEAT]),
            "b_n1": sb("b_n1", [P, 1]),
            "ones3": sb("ones3", [3, P], BF16),
            "bias3": sb("bias3", [3, 4 * HID], BF16),
            "base_row": sb("base_row", [1, sh.blocks * P], I32),
            "flag": sb("flag", [1, 1], I32),
        }
        prepare(nc, sh, keep, x, src, dst, Wo1, bo1, Wo2, bo2, Wi1, bi1, Wi2, bi2, Wn1, bn1, Wn2, bn2,
                proj, row_keys, bases, tables)
        edge_phase(nc, sh, keep, ea, proj, row_keys, tables)
        node_phase(nc, sh, keep, tables, out)


B_SECOND = 0
B_FIRST = 2 * FEAT
B_NODE = B_FIRST + 2 * HID
B_END = B_NODE + FEAT

STEP = 7


def prepare(nc, sh, keep, x, src, dst, Wo1, bo1, Wo2, bo2, Wi1, bi1, Wi2, bi2, Wn1, bn1, Wn2, bn2,
            proj, row_keys, bases, tables):
    x_all, cols, ident, tri, pid, spare = (keep[k] for k in ("x_all", "cols", "ident", "tri", "pid", "spare"))
    NB, J = sh.blocks, sh.per_part
    steps = J // STEP
    assert J % STEP == 0
    full = P - 1
    tail = sh.nodes - full * J
    whole = (sh.groups - 1) // P
    odd = sh.groups - 1 - whole * P
    zero_runs = 2 * STEP
    zero_len = sh.slots * FEAT // P // zero_runs

    with ExitStack() as ctx:
        def sb(name, shape, dt=F32):
            return ctx.enter_context(nc.sbuf_tensor(name, shape, dt))

        def sem(name):
            return ctx.enter_context(nc.semaphore(name))

        src_i = sb("src_i", [P, NB, GROUP], I32)
        dst_i = sb("dst_i", [P, NB, GROUP], I32)
        slot_r = sb("slot_r", [P, NB, GROUP])
        in_r = sb("in_r", [P, NB, GROUP])
        out_r = sb("out_r", [P, NB, GROUP])
        key_r = src_i[:].bitcast(F32)
        rows_u = sb("rows_u", [P, NB, 2, GROUP], U16)
        dmin = sb("dmin", [P, NB])
        dmax = sb("dmax", [P, NB])
        base2 = sb("base2", [P, NB])
        base_i = sb("base_i", [P, NB], I32)
        wide = sb("wide", [P, NB])
        wide1 = sb("wide1", [P, 1])
        wide_all = sb("wide_all", [1, 1])
        zeros = sb("zeros", [P, zero_len])
        w_node = sb("w_node", [FEAT, 2 * HID])
        b_row = sb("b_row", [1, 4 * HID])
        b_rest = sb("b_rest", [1, 4 * HID])
        b_parts = sb("b_parts", [1, 3, 4 * HID], BF16)
        eps = sb("eps", [P, 1])
        mean = sb("mean", [P, J])
        var = sb("var", [P, J])
        rstd = sb("rstd", [P, J])
        squares = sb("squares", [P, STEP, FEAT])
        centred = sb("centred", [P, STEP, FEAT])
        normed = sb("normed", [P, STEP, FEAT])
        hT = sb("hT", [FEAT, STEP, P])
        proj_sb = sb("proj_sb", [P, STEP, 2 * HID])

        ps_hT = ctx.enter_context(nc.psum_tensor("ps_hT", [P, 2 * 512], F32))
        ps_proj = ctx.enter_context(nc.psum_tensor("ps_proj", [P, 4 * 512], F32))
        ps_col = ctx.enter_context(nc.psum_tensor("ps_col", [P, 2 * 512], F32))

        weights_in = sem("weights_in")
        x_in = sem("x_in")
        ids_in = sem("ids_in")
        const_made = sem("const_made")
        zero_made = sem("zero_made")
        tables_zeroed = sem("tables_zeroed")
        clean = sem("clean")
        chain = sem("chain")
        biases_split = sem("biases_split")
        biases_in = sem("biases_in")
        spread = sem("spread")
        centre_done = sem("centre_done")
        recentre = sem("recentre")
        rooted = sem("rooted")
        normed_made = sem("normed_made")
        hT_tr = sem("hT_tr")
        hT_made = sem("hT_made")
        proj_done = sem("proj_done")
        proj_copied = sem("proj_copied")
        proj_stored = sem("proj_stored")
        rows_made = sem("rows_made")
        rows_stored = sem("rows_stored")
        bases_out = sem("bases_out")
        bases_in = sem("bases_in")
        fields_made = sem("fields_made")
        col_tr = sem("col_tr")
        col_copied = sem("col_copied")
        flag_tr = sem("flag_tr")

        block = ctx.enter_context(nc.Block())

        N_WEIGHTS = 15
        cuts = [(0, 112), (112, full)]

        @block.sync
        def _(sp):
            sp.wait_ge(clean, 3)
            for a, b in cuts:
                sp.dma_start(x_all[a:b, :, :], x[a * J:b * J, :].rearrange("(p j) f -> p j f", j=J)).then_inc(x_in, 16)
            sp.dma_start(x_all[full:P, 0:tail, :],
                         x[full * J:sh.nodes, :].rearrange("(p j) f -> p j f", p=1)).then_inc(x_in, 16)
            for ids, ids_i in ((src, src_i), (dst, dst_i)):
                sp.dma_start(ids_i[:, 0:whole, :],
                             ids[0:whole * P * GROUP].rearrange("(b q e) -> q b e", q=P, e=GROUP)).then_inc(ids_in, 16)
                sp.dma_start(ids_i[0:odd, whole, :],
                             ids[whole * P * GROUP:(whole * P + odd) * GROUP].rearrange("(q e) -> q e", e=GROUP)
                             ).then_inc(ids_in, 16)
                sp.dma_start(ids_i[odd:odd + 1, whole, :],
                             ids[sh.last_e0:sh.edges].rearrange("(q e) -> q e", q=1)).then_inc(ids_in, 16)
            sp.wait_ge(zero_made, 1)
            for table in tables:
                sp.dma_start(table[0:sh.slots, :].rearrange("(p c r) f -> p c (r f)", p=P, c=zero_runs),
                             zeros[:].unsqueeze(1).to_broadcast([P, zero_runs, zero_len])).then_inc(tables_zeroed, 16)
                sp.dma_start(table[sh.slots:sh.slots + P, :], zeros[:, 0:FEAT]).then_inc(tables_zeroed, 16)
            sp.wait_ge(rows_made, 1)
            sp.dma_start(row_keys.rearrange("(b q) k -> q b k", q=P),
                         rows_u[:].rearrange("q b k e -> q b (k e)")).then_inc(rows_stored, 16)
            with nc.allow_non_contiguous_dma(reason="one base a group, once"):
                sp.dma_start(bases.rearrange("b q -> q b"), base_i[:]).then_inc(bases_out, 16)
            sp.wait_ge(bases_out, 16)
            sp.dma_start(keep["base_row"][:], bases.rearrange("(a b) q -> a (b q)", a=1)).then_inc(bases_in, 16)
            sp.wait_ge(rows_stored, 16)
            sp.wait_ge(bases_in, 16)
            sp.wait_ge(tables_zeroed, 16 * 2 * TILES)

        @block.gpsimd
        def _(pool):
            pool.memset(zeros[:], 0.0).then_inc(zero_made, 1)
            pool.memset(ident[:], 0.0).then_inc(spread, 1)
            pool.memset(tri[:], 1.0).then_inc(spread, 1)
            pool.memset(keep["ones3"][:], 1.0).then_inc(const_made, 1)
            pool.memset(b_row[:], 0.0).then_inc(const_made, 1)
            pool.memset(eps[:], EPS).then_inc(const_made, 1)
            pool.iota(pid[:], pattern=[[0, 1]], base=0, channel_multiplier=1,
                      allow_small_or_imprecise_dtypes=True).then_inc(const_made, 1)
            pool.iota(spare[:], pattern=[[0, 1]], base=sh.slots, channel_multiplier=1,
                      allow_small_or_imprecise_dtypes=True).then_inc(const_made, 1)
            pool.wait_ge(spread, 2)
            pool.affine_select(out=ident[:], in_=ident[:], compare_op=ALU.not_equal, fill=1.0, base=0,
                               pattern=[[-1, P]], channel_multiplier=1).then_inc(const_made, 1)
            pool.affine_select(out=tri[:], in_=tri[:], compare_op=ALU.is_ge, fill=0.0, base=0,
                               pattern=[[1, P]], channel_multiplier=-1).then_inc(const_made, 1)

        N_CONST = 7

        @block.scalar
        def _(act):
            for dst_ap, src_ap in (
                (w_node[:, 0:HID], Wi1[0:FEAT, :]), (w_node[:, HID:2 * HID], Wo1[0:FEAT, :]),
                (keep["w_edge"][0:FEAT, :], Wi1[FEAT:2 * FEAT, :]), (keep["w_edge"][FEAT:P, :], Wo1[FEAT:2 * FEAT, :]),
                (keep["w_second"][:, 0:FEAT], Wi2), (keep["w_second"][:, FEAT:2 * FEAT], Wo2),
                (keep["w_n1"][:], Wn1), (keep["w_n2"][:], Wn2),
                (keep["b_n1"][:], bn1.rearrange("(p a) -> p a", a=1)),
            ):
                act.dma_start(dst_ap, src_ap).then_inc(weights_in, 16)
            act.wait_ge(const_made, 2)
            for at, b in ((B_SECOND, bi2), (B_SECOND + FEAT, bo2), (B_FIRST, bi1), (B_FIRST + HID, bo1), (B_NODE, bn2)):
                act.dma_start(b_row[:, at:at + b.shape[0]], b.rearrange("(a n) -> a n", a=1)).then_inc(weights_in, 16)
            act.wait_ge(biases_split, 3)
            for k in range(3):
                act.dma_start(keep["bias3"][k:k + 1, :], b_parts[:, k, :]).then_inc(biases_in, 16)
            act.wait_ge(centre_done, 3 * steps)
            act.wait_ge(const_made, N_CONST)
            act.activation(rstd[:], var[:], ACT.Sqrt, scale=1.0 / FEAT, bias=eps[:]).then_inc(rooted, 1)
            with act.Fori(0, steps) as s:
                act.wait_ge(hT_tr, s + 1)
                act.wait_ge(proj_done, s)
                act.activation(hT[:, 0:4, :], ps_hT[0:FEAT, 0:512].rearrange("p (t n) -> p t n", n=P), ACT.Relu)
                act.activation(hT[:, 4:STEP, :], ps_hT[0:FEAT, 512:512 + (STEP - 4) * P]
                               .rearrange("p (t n) -> p t n", n=P), ACT.Relu).then_inc(hT_made, 1)
                act.wait_ge(proj_done, s + 1)
                act.wait_ge(proj_stored, s * 16)
                act.activation(proj_sb[:].rearrange("p t n -> p (t n)"), ps_proj[:, 0:STEP * 2 * HID],
                               ACT.Copy).then_inc(proj_copied, 1)
                act.wait_ge(proj_copied, s + 1)
                act.dma_start(proj.rearrange("(p j) n -> p (j n)", j=J)[:, bass.ds(s * (STEP * 2 * HID), STEP * 2 * HID)],
                              proj_sb[:].rearrange("p t n -> p (t n)")).then_inc(proj_stored, 16)
            act.wait_ge(proj_stored, 16 * steps)

        @block.vector
        def _(dve):
            links = [0]

            def link(ins):
                links[0] += 1
                ins.then_inc(chain, 1)
                dve.wait_ge(chain, links[0])

            nc.vector.memset(x_all[96:P, :, :], 0.0).then_inc(clean, 1)
            nc.vector.memset(src_i[:, NB - 1, :], 0).then_inc(clean, 1)
            nc.vector.memset(dst_i[:, NB - 1, :], 0).then_inc(clean, 1)

            dve.wait_ge(weights_in, 16 * 14)
            nc.vector.tensor_copy(b_parts[:, 0, :], b_row[:]).then_inc(biases_split, 1)
            dve.wait_ge(biases_split, 1)
            link(nc.vector.tensor_tensor(b_rest[:], b_row[:], b_parts[:, 0, :], ALU.subtract))
            nc.vector.tensor_copy(b_parts[:, 1, :], b_rest[:]).then_inc(biases_split, 1)
            dve.wait_ge(biases_split, 2)
            link(nc.vector.tensor_tensor(b_rest[:], b_rest[:], b_parts[:, 1, :], ALU.subtract))
            nc.vector.tensor_copy(b_parts[:, 2, :], b_rest[:]).then_inc(biases_split, 1)

            dve.wait_ge(x_in, 16 * 3)
            link(nc.vector.tensor_reduce(mean[:], x_all[:], AX_X, ALU.add))
            link(nc.vector.tensor_scalar(mean[:], mean[:], 1.0 / FEAT, None, ALU.mult))
            with dve.Fori(0, steps) as s:
                nodes = bass.ds(s * STEP, STEP)
                dve.wait_ge(centre_done, s * 3)
                nc.vector.tensor_tensor(centred[:], x_all[:, nodes, :],
                                        mean[:, nodes].unsqueeze(2).to_broadcast([P, STEP, FEAT]),
                                        ALU.subtract).then_inc(centre_done, 1)
                dve.wait_ge(centre_done, s * 3 + 1)
                nc.vector.tensor_tensor(squares[:], centred[:], centred[:], ALU.mult).then_inc(centre_done, 1)
                dve.wait_ge(centre_done, s * 3 + 2)
                nc.vector.tensor_reduce(var[:, nodes], squares[:], AX_X, ALU.add).then_inc(centre_done, 1)
            dve.wait_ge(rooted, 1)
            link(nc.vector.reciprocal(rstd[:], rstd[:]))
            with dve.Fori(0, steps) as s:
                nodes = bass.ds(s * STEP, STEP)
                dve.wait_ge(normed_made, s)
                nc.vector.tensor_tensor(centred[:], x_all[:, nodes, :],
                                        mean[:, nodes].unsqueeze(2).to_broadcast([P, STEP, FEAT]),
                                        ALU.subtract).then_inc(recentre, 1)
                dve.wait_ge(recentre, s + 1)
                dve.wait_ge(hT_tr, s)
                nc.vector.tensor_tensor(normed[:], centred[:],
                                        rstd[:, nodes].unsqueeze(2).to_broadcast([P, STEP, FEAT]),
                                        ALU.mult).then_inc(normed_made, 1)

            dve.wait_ge(ids_in, 16 * 6)
            dve.wait_ge(const_made, N_CONST)
            nc.vector.tensor_tensor(out_r[:], src_i[:], dst_i[:], ALU.is_lt)
            link(nc.vector.tensor_tensor(in_r[:], src_i[:], dst_i[:], ALU.is_gt))
            link(nc.vector.scalar_tensor_tensor(slot_r[:], src_i[:], 2.0, out_r[:], ALU.mult, ALU.add))
            link(nc.vector.scalar_tensor_tensor(key_r, dst_i[:], 2.0, out_r[:], ALU.mult, ALU.add))
            nc.vector.tensor_reduce(dmin[:], dst_i[:], AX_X, ALU.min)
            link(nc.vector.tensor_reduce(dmax[:], dst_i[:], AX_X, ALU.max))
            link(nc.vector.tensor_scalar(dmin[:], dmin[:], float(sh.padded - WINDOW), None, ALU.min))
            nc.vector.tensor_copy(base_i[:], dmin[:])
            link(nc.vector.tensor_scalar(base2[:], dmin[:], 2.0, None, ALU.mult))
            nc.vector.tensor_tensor(wide[:], dmax[:], dmin[:], ALU.subtract)
            for b in range(NB):
                nc.vector.tensor_copy(rows_u[:, b, 0, :].rearrange("q (t p) -> q p t", t=TILES),
                                      slot_r[:, b, :].rearrange("q (p t) -> q p t", t=TILES))
                last = nc.vector.tensor_scalar(rows_u[:, b, 1, :].rearrange("q (t p) -> q p t", t=TILES),
                                               key_r[:, b, :].rearrange("q (p t) -> q p t", t=TILES),
                                               base2[:, b:b + 1], None, ALU.subtract)
            last.then_inc(rows_made, 1)
            dve.wait_ge(rows_made, 1)
            nc.vector.tensor_reduce(wide1[:], wide[:], AX_X, ALU.max).then_inc(fields_made, 1)
            dve.wait_ge(flag_tr, 1)
            link(nc.vector.tensor_reduce(wide_all[:], ps_hT[0:1, 0:P], AX_X, ALU.max))
            link(nc.vector.tensor_scalar(keep["flag"][:], wide_all[:], float(WINDOW - 1), None, ALU.is_gt))

            n = 0
            for b in range(NB):
                q = min(P, sh.groups - b * P)
                for kind in (C_SLOT, C_IN, C_OUT, C_KEY):
                    dve.wait_ge(col_tr, n + 1)
                    got = ps_col[:, 512 * (n % 2):512 * (n % 2) + 512].rearrange("p (t q) -> p q t", t=TILES)[:, 0:q, :]

                    def field(k):
                        return cols[:, b * P:b * P + q, k]
                    if kind == C_SLOT:
                        nc.vector.tensor_scalar(field(C_REL), got, spare[:, 0:1], None, ALU.subtract)
                    nc.vector.tensor_copy(field(kind), got).then_inc(col_copied, 1)
                    n += 1
            dve.wait_ge(col_copied, n)
            link(nc.vector.memset(cols[0:sh.repeated // TILES, sh.groups - 1, C_MASKS], 0.0))

        @block.tensor
        def _(pe):
            pe.wait_ge(const_made, N_CONST)
            pe.wait_ge(weights_in, 16 * 14)
            pe.wait_ge(biases_in, 16 * 3)
            held = pe.alloc_register("held")
            with pe.Fori(0, steps) as s:
                due = s + 1
                pe.reg_mov(held, due)
                pe.wait_ge(normed_made, 1)
                pe.wait_ge(normed_made, due)
                pe.wait_ge(hT_made, s)
                for t in range(STEP):
                    last = nc.tensor.transpose(ps_hT[0:FEAT, t * P:(t + 1) * P], normed[:, t, :], ident[:])
                last.then_inc(hT_tr, 1)
                pe.wait_ge(hT_made, s + 1)
                pe.wait_ge(proj_copied, s)
                for t in range(STEP):
                    o = ps_proj[:, t * 2 * HID:(t + 1) * 2 * HID]
                    nc.tensor.matmul(o, keep["ones3"][:], keep["bias3"][:, B_FIRST:B_FIRST + 2 * HID],
                                     start=True, stop=False)
                    last = nc.tensor.matmul(o, hT[:, t, :], w_node[:], start=False, stop=True)
                last.then_inc(proj_done, 1)
            pe.wait_ge(fields_made, 1)
            pe.wait_ge(hT_made, steps)
            nc.tensor.transpose(ps_hT[0:1, 0:P], wide1[:], ident[:]).then_inc(flag_tr, 1)
            n = 0
            for b in range(NB):
                for field in (slot_r[:], in_r[:], out_r[:], key_r):
                    if n >= 2:
                        pe.wait_ge(col_copied, n - 1)
                    for t in range(TILES):
                        last = nc.tensor.transpose(ps_col[:, 512 * (n % 2) + t * P:512 * (n % 2) + (t + 1) * P],
                                                   field[:, b, :].rearrange("q (p t) -> q t p", t=TILES)[:, t, :],
                                                   ident[:])
                    last.then_inc(col_tr, 1)
                    n += 1


class Group:

    def __init__(self, it, s):
        self.n = it * 4 + s
        self.ring4, self.ring2 = s % 4, s % 2
        self.turn = it + s // 4


def run_steps(eng, groups, lag, step):
    turns = groups // 4
    for i in range(8):
        step(0, i)
    with eng.Fori(2, turns) as it:
        for s in range(4):
            step(it, s)
    for s in range(groups + lag - 4 * turns):
        step(turns, s)


def edge_phase(nc, sh, keep, ea, proj, row_keys, tables):
    cols, ident, tri, pid, spare = (keep[k] for k in ("cols", "ident", "tri", "pid", "spare"))
    G = sh.groups
    LAG = 3

    with ExitStack() as ctx:
        def sb(name, shape, dt=F32):
            return ctx.enter_context(nc.sbuf_tensor(name, shape, dt))

        def ps(name, shape):
            return ctx.enter_context(nc.psum_tensor(name, shape, F32))

        def sem(name):
            return ctx.enter_context(nc.semaphore(name))

        edges_sb = sb("edges_sb", [P, 4, TILES, FEAT])
        keys_sb = sb("keys_sb", [P, 4, 2, GROUP], U16)
        window = sb("window", [P, 4, HID])
        col = sb("col", [P, 4, FIELDS])
        masked = sb("masked", [P, 2, TILES, 2, FEAT])
        onehot = sb("onehot", [P, 2, GROUP])
        same = sb("same", [P, 4, TILES, P])
        later = sb("later", [P, 4, TILES])
        kept = sb("kept", [P, 2, TILES])
        slot_u = sb("slot_u", [P, 2, TILES], U32)
        key_u = sb("key_u", [P, 2, TILES], U32)
        picked = sb("picked", [P, 2, TILES, HID])
        maskedT = sb("maskedT", [P, 2, GROUP])
        hidden = sb("hidden", [P, 2, GROUP])
        both = sb("both", [P, 2, TILES, 2, FEAT])
        message = sb("message", [P, 2, TILES, FEAT])
        flow_sb = sb("flow_sb", [P, 2, TILES, FEAT])

        ps_t = ps("ps_t", [P, 2, 512])
        ps_h = ps("ps_h", [P, 2, 512])
        ps_z = ps("ps_z", [P, 2, 512])
        ps_f = ps("ps_f", [P, 2, 512])

        edges_in = [sem(f"edges_in{r}") for r in range(4)]
        keys_in = [sem(f"keys_in{r}") for r in range(4)]
        window_in = [sem(f"window_in{r}") for r in range(4)]
        picked_in = [sem(f"picked_in{r}") for r in range(2)]
        added = [sem(f"added{t}") for t in range(TILES)]
        col_made = sem("col_made")
        masked_made = sem("masked_made")
        onehot_made = sem("onehot_made")
        key_made = sem("key_made")
        same_made = sem("same_made")
        kept_made = sem("kept_made")
        slot_made = sem("slot_made")
        both_made = sem("both_made")
        message_made = sem("message_made")
        transposed = sem("transposed")
        maskedT_made = sem("maskedT_made")
        first_done = sem("first_done")
        hidden_made = sem("hidden_made")
        second_done = sem("second_done")
        summed = sem("summed")
        flow_made = sem("flow_made")

        block = ctx.enter_context(nc.Block())

        def each_path(eng, program):
            with eng.register("wide_flag") as flag:
                eng.reg_load(flag, keep["flag"][0:1, 0:1])
                with eng.If_eq(flag, 0):
                    program(False)
                with eng.Else():
                    program(True)

        @block.sync
        def _(sp):
            def program(general):
                def load(it, s):
                    g = Group(it, s)
                    i = g.n
                    static = isinstance(i, int)
                    r = g.ring4
                    e0 = min(i * GROUP, sh.last_e0) if static else i * GROUP
                    if not static or i >= 4:
                        sp.wait_ge(masked_made, i - 3)
                    sp.dma_start(edges_sb[:, r, :, :].rearrange("p t f -> p (t f)"),
                                 ea[bass.ds(e0, GROUP), :].rearrange("(p t) f -> p (t f)", t=TILES)
                                 ).then_inc(edges_in[r], 16)
                    if not static or i >= 4:
                        sp.wait_ge(same_made, i - 3)
                        if not general:
                            sp.wait_ge(onehot_made, i - 3)
                    sp.dma_start(keys_sb[:, r, :, :].rearrange("p k e -> p (k e)"),
                                 row_keys[bass.ds(i, 1), :].to_broadcast([P, 2 * GROUP])).then_inc(keys_in[r], 16)
                    if not general:
                        base = sp.value_load(keep["base_row"][0:1, bass.ds(i, 1)], min_val=0,
                                             max_val=sh.padded - WINDOW)
                        if not static or i >= 4:
                            sp.wait_ge(first_done, i - 3)
                        sp.dma_start(window[:, r, :],
                                     proj[bass.ds(base, WINDOW), :].rearrange("n (d h) -> (n d) h", d=2)
                                     ).then_inc(window_in[r], 16)
                run_steps(sp, G, 0, load)
            each_path(sp, program)

        @block.vector
        def _(dve):
            def program(general):
                def step(it, s):
                    g, d = Group(it, s), Group(it, s - LAG)
                    i, j = g.n, d.n
                    static = isinstance(i, int)
                    front, back = not static or i < G, not static or 0 <= j < G
                    old = not static or i >= 4
                    r = g.ring4
                    if front:
                        if old:
                            dve.wait_ge(kept_made, i - 3)
                        nc.vector.tensor_copy(col[:, r, :],
                                              cols[:, bass.ds(i, 1), :].rearrange("p a k -> p (a k)")
                                              ).then_inc(col_made, 1)
                    if back:
                        dve.wait_ge(second_done, j + 1)
                        if not static or j >= 2:
                            dve.wait_ge(message_made, j - 1)
                        nc.vector.scalar_tensor_tensor(
                            both[:, d.ring2, :, :, :].rearrange("p t d f -> p (t d) f"),
                            ps_z[:, d.ring2, :].rearrange("p (m f) -> p m f", f=FEAT), 0.0,
                            col[:, d.ring4, C_MASKS].unsqueeze(2).to_broadcast([P, 2 * TILES, FEAT]),
                            ALU.max, ALU.mult).then_inc(both_made, 1)
                    if front:
                        dve.wait_ge(col_made, i + 1)
                        dve.wait_ge(edges_in[r], 16 * (g.turn + 1))
                        if old or i >= 2:
                            dve.wait_ge(transposed, i - 1)
                        nc.vector.tensor_tensor(
                            masked[:, g.ring2, :, :, :],
                            edges_sb[:, r, :, :].unsqueeze(2).to_broadcast([P, TILES, 2, FEAT]),
                            col[:, r, C_MASKS].rearrange("p (t d) -> p t d", d=2).unsqueeze(3)
                            .to_broadcast([P, TILES, 2, FEAT]), ALU.mult).then_inc(masked_made, 1)
                        dve.wait_ge(keys_in[r], 16 * (g.turn + 1))
                        if old:
                            dve.wait_ge(summed, i - 3)
                        for t in range(TILES):
                            last = nc.vector.scalar_tensor_tensor(
                                same[:, r, t, :], keys_sb[:, r, 0, t * P:(t + 1) * P], col[:, r, t:t + 1],
                                tri[:], ALU.is_equal, ALU.mult, accum_out=later[:, r, t:t + 1])
                        last.then_inc(same_made, 1)
                    if back:
                        dve.wait_ge(both_made, j + 1)
                        if not static or j >= 2:
                            dve.wait_ge(summed, j - 1)
                        nc.vector.tensor_tensor(message[:, d.ring2, :, :], both[:, d.ring2, :, 0, :],
                                                both[:, d.ring2, :, 1, :], ALU.add).then_inc(message_made, 1)
                        dve.wait_ge(same_made, j + 1)
                        if not static or j >= 2:
                            dve.wait_ge(slot_made, j - 1)
                        nc.vector.scalar_tensor_tensor(
                            kept[:, d.ring2, :], later[:, d.ring4, :], 1.0, col[:, d.ring4, C_REL],
                            ALU.is_equal, ALU.mult).then_inc(kept_made, 1)
                    if front:
                        if general:
                            if not static or i >= 2:
                                for_ring = 16 * TILES
                                dve.wait_ge(picked_in[g.ring2], for_ring * (i // 2) if static else for_ring * (it * 2 + s // 2))
                            nc.vector.tensor_copy(key_u[:, g.ring2, :], col[:, r, C_KEY]).then_inc(key_made, 1)
                        else:
                            if not static or i >= 2:
                                dve.wait_ge(first_done, i - 1)
                            nc.vector.tensor_scalar(onehot[:, g.ring2, :], keys_sb[:, r, 1, :], pid[:, 0:1], None,
                                                    ALU.is_equal).then_inc(onehot_made, 1)
                    if back:
                        dve.wait_ge(kept_made, j + 1)
                        if not static or j >= 2:
                            for t in range(TILES):
                                dve.wait_ge(added[t], 16 * (j - 1))
                        nc.vector.tensor_scalar(slot_u[:, d.ring2, :], kept[:, d.ring2, :], spare[:, 0:1], None,
                                                ALU.add).then_inc(slot_made, 1)
                run_steps(dve, G, LAG, step)
            each_path(dve, program)

        @block.tensor
        def _(pe):
            def program(general):
                def step(it, s):
                    a, b, c, d = (Group(it, s - k) for k in range(4))
                    static = isinstance(a.n, int)

                    def on(g):
                        return not static or 0 <= g.n < G
                    if on(a):
                        pe.wait_ge(masked_made, a.n + 1)
                        if not static or a.n >= 2:
                            pe.wait_ge(maskedT_made, a.n - 1)
                        for t in range(TILES):
                            last = nc.tensor.transpose(
                                ps_t[:, a.ring2, t * P:(t + 1) * P],
                                masked[:, a.ring2, t, :, :].rearrange("p d f -> p (d f)"), ident[:])
                        last.then_inc(transposed, 1)
                    if on(c):
                        pe.wait_ge(hidden_made, c.n + 1)
                        if not static or c.n >= 2:
                            pe.wait_ge(both_made, c.n - 1)
                        nc.tensor.matmul(
                            ps_z[:, c.ring2, :].rearrange("p (t n) -> p t n", t=TILES), keep["ones3"][:],
                            keep["bias3"][:, B_SECOND:B_SECOND + 2 * FEAT].unsqueeze(1).to_broadcast([3, TILES, 2 * FEAT]),
                            start=True, stop=False)
                        for t in range(TILES):
                            last = nc.tensor.matmul(
                                ps_z[:, c.ring2, t * P:(t + 1) * P], hidden[:, c.ring2, t * P:(t + 1) * P],
                                keep["w_second"][:], start=False, stop=(t == TILES - 1))
                        last.then_inc(second_done, 1)
                    if on(b):
                        pe.wait_ge(maskedT_made, b.n + 1)
                        if not static or b.n >= 2:
                            pe.wait_ge(hidden_made, b.n - 1)
                        nc.tensor.matmul(ps_h[:, b.ring2, :], keep["w_edge"][:], maskedT[:, b.ring2, :],
                                         start=True, stop=False)
                        if general:
                            rounds = b.n // 2 if static else it * 2 + (s - 1) // 2
                            pe.wait_ge(picked_in[b.ring2], 16 * TILES * (rounds + 1))
                            for t in range(TILES):
                                last = nc.tensor.matmul(ps_h[:, b.ring2, t * P:(t + 1) * P],
                                                        picked[:, b.ring2, t, :], ident[:],
                                                        start=False, stop=(t == TILES - 1))
                        else:
                            pe.wait_ge(window_in[b.ring4], 16 * (b.turn + 1))
                            pe.wait_ge(onehot_made, b.n + 1)
                            last = nc.tensor.matmul(ps_h[:, b.ring2, :], window[:, b.ring4, :],
                                                    onehot[:, b.ring2, :], start=False, stop=True)
                        last.then_inc(first_done, 1)
                    if on(d):
                        pe.wait_ge(message_made, d.n + 1)
                        pe.wait_ge(same_made, d.n + 1)
                        if not static or d.n >= 2:
                            pe.wait_ge(flow_made, d.n - 1)
                        for t in range(TILES):
                            last = nc.tensor.matmul(ps_f[:, d.ring2, t * FEAT:(t + 1) * FEAT], same[:, d.ring4, t, :],
                                                    message[:, d.ring2, t, :], start=True, stop=True)
                        last.then_inc(summed, 1)
                run_steps(pe, G, LAG, step)
            each_path(pe, program)

        @block.scalar
        def _(act):
            def program(general):
                def step(it, s):
                    a, b, d = Group(it, s), Group(it, s - 1), Group(it, s - 3)
                    static = isinstance(a.n, int)

                    def on(g):
                        return not static or 0 <= g.n < G
                    if on(a):
                        act.wait_ge(transposed, a.n + 1)
                        if not static or a.n >= 2:
                            act.wait_ge(first_done, a.n - 1)
                        act.activation(maskedT[:, a.ring2, :], ps_t[:, a.ring2, :], ACT.Copy).then_inc(maskedT_made, 1)
                    if on(b):
                        act.wait_ge(first_done, b.n + 1)
                        if not static or b.n >= 2:
                            act.wait_ge(second_done, b.n - 1)
                        act.activation(hidden[:, b.ring2, :], ps_h[:, b.ring2, :], ACT.Relu).then_inc(hidden_made, 1)
                    if on(d):
                        act.wait_ge(summed, d.n + 1)
                        if not static or d.n >= 2:
                            for t in range(TILES):
                                act.wait_ge(added[t], 16 * (d.n - 1))
                        act.activation(flow_sb[:, d.ring2, :, :].rearrange("p t f -> p (t f)"),
                                       ps_f[:, d.ring2, 0:TILES * FEAT], ACT.Copy).then_inc(flow_made, 1)
                run_steps(act, G, LAG, step)
            each_path(act, program)

        @block.gpsimd
        def _(pool):
            held = pool.alloc_register("held")

            def value(v):
                if not isinstance(v, int):
                    pool.reg_mov(held, v)
                return v

            def program(general):
                def step(it, s):
                    g, d = Group(it, s), Group(it, s - LAG)
                    static = isinstance(g.n, int)
                    if general and (not static or g.n < G):
                        keys_due, free_due = value(g.n + 1), value(g.n - 1)
                        pool.wait_ge(key_made, 1)
                        pool.wait_ge(key_made, keys_due)
                        if not static or g.n >= 2:
                            pool.wait_ge(first_done, free_due)
                        for t in range(TILES):
                            pool.indirect_dma_start(
                                out=picked[:, g.ring2, t, :], out_offset=None,
                                in_=proj.rearrange("n (d h) -> (n d) h", d=2),
                                in_offset=bass.IndirectOffsetOnAxis(ap=key_u[:, g.ring2, t:t + 1], axis=0),
                            ).then_inc(picked_in[g.ring2], 16)
                    if not static or 0 <= d.n < G:
                        due, added_due = value(d.n + 1), value(16 * d.n)
                        pool.wait_ge(flow_made, 1)
                        pool.wait_ge(flow_made, due)
                        pool.wait_ge(slot_made, due)
                        for t in range(TILES):
                            if not static or d.n >= 1:
                                if t:
                                    pool.wait_ge(flow_made, 1)
                                pool.wait_ge(added[t], added_due)
                            pool.indirect_dma_start(
                                out=tables[t],
                                out_offset=bass.IndirectOffsetOnAxis(ap=slot_u[:, d.ring2, t:t + 1], axis=0),
                                in_=flow_sb[:, d.ring2, t, :], in_offset=None, compute_op=ALU.add,
                            ).then_inc(added[t], 16)
                run_steps(pool, G, LAG, step)
            each_path(pool, program)
            for t in range(TILES):
                pool.wait_ge(added[t], 16 * G)


def node_phase(nc, sh, keep, tables, out):
    x_all, ident = keep["x_all"], keep["ident"]
    J = sh.per_part
    steps = J // STEP
    LOT = STEP * 2 * FEAT
    HALF = 4
    full = P - 1
    tail = sh.nodes - full * J

    with ExitStack() as ctx:
        def sb(name, shape, dt=F32):
            return ctx.enter_context(nc.sbuf_tensor(name, shape, dt))

        def ps(name, shape):
            return ctx.enter_context(nc.psum_tensor(name, shape, F32))

        def sem(name):
            return ctx.enter_context(nc.semaphore(name))

        parts = sb("parts", [P, 2, TILES, LOT])
        pairs = sb("pairs", [P, 2, LOT])
        flow = sb("flow", [P, STEP, 2 * FEAT])
        flowT = sb("flowT", [P, STEP * P])
        hid = sb("hid", [P, STEP * P])
        outs = sb("outs", [P, J, FEAT])

        ps_flow = ps("ps_flow", [P, 2 * 512])
        ps_hid = ps("ps_hid", [P, 2 * 512])
        ps_out = ps("ps_out", [P, 512])

        parts_in = [sem(f"parts_in{r}") for r in range(2)]
        pair_made = sem("pair_made")
        flow_made = sem("flow_added")
        flow_tr = sem("flow_tr")
        flowT_made = sem("flowT_made")
        hid_done = sem("hid_done")
        hid_made = sem("hid_made")
        out_done = sem("out_done")
        out_made = sem("out_made")
        out_stored = sem("out_stored")

        block = ctx.enter_context(nc.Block())
        flat = [t[0:sh.slots, :].rearrange("(p j) f -> p (j f)", p=P) for t in tables]

        @block.sync
        def _(sp):
            with sp.Fori(0, steps // 2) as it:
                for r in range(2):
                    s = it * 2 + r
                    for t in range(TILES):
                        if t == 0:
                            sp.wait_ge(pair_made, 2 * it * 2)
                        sp.dma_start(parts[:, r, t, :], flat[t][:, bass.ds(s * LOT, LOT)]).then_inc(parts_in[r], 16)
                    if r == 0:
                        sp.wait_ge(flow_made, it * 2)
            sp.wait_ge(out_made, steps)
            for a, b in ((0, 112), (112, full)):
                sp.dma_start(out[a * J:b * J, :].rearrange("(p j) f -> p j f", j=J), outs[a:b, :, :]).then_inc(out_stored, 16)
            sp.dma_start(out[full * J:sh.nodes, :].rearrange("(p j) f -> p j f", p=1),
                         outs[full:P, 0:tail, :]).then_inc(out_stored, 16)
            sp.wait_ge(out_stored, 16 * 3)

        @block.vector
        def _(dve):
            with dve.Fori(0, steps // 2) as it:
                for r in range(2):
                    s = it * 2 + r
                    dve.wait_ge(parts_in[r], (it + 1) * (16 * TILES))
                    dve.wait_ge(flow_made, s)
                    for h in range(2):
                        nc.vector.tensor_tensor(pairs[:, h, :], parts[:, r, 2 * h, :], parts[:, r, 2 * h + 1, :],
                                                ALU.add).then_inc(pair_made, 1)
                    dve.wait_ge(pair_made, s * 2 + 2)
                    dve.wait_ge(flow_tr, s)
                    nc.vector.tensor_tensor(flow[:].rearrange("p t n -> p (t n)"), pairs[:, 0, :], pairs[:, 1, :],
                                            ALU.add).then_inc(flow_made, 1)
                    dve.wait_ge(out_done, s + 1)
                    nc.vector.scalar_tensor_tensor(
                        outs[:, bass.ds(s * STEP, STEP), :], ps_out[:, 0:STEP * FEAT].rearrange("p (t f) -> p t f", f=FEAT),
                        0.0, x_all[:, bass.ds(s * STEP, STEP), :], ALU.max, ALU.add).then_inc(out_made, 1)

        @block.tensor
        def _(pe):
            with pe.Fori(0, steps) as s:
                pe.wait_ge(flow_made, s + 1)
                pe.wait_ge(flowT_made, s)
                for t in range(STEP):
                    last = nc.tensor.transpose(ps_flow[:, t * P:(t + 1) * P], flow[:, t, :], ident[:])
                last.then_inc(flow_tr, 1)
                pe.wait_ge(flowT_made, s + 1)
                pe.wait_ge(hid_made, s)
                nc.tensor.matmul(ps_hid[:, 0:HALF * P], keep["w_n1"][:], flowT[:, 0:HALF * P], start=True, stop=True)
                nc.tensor.matmul(ps_hid[:, HALF * P:STEP * P], keep["w_n1"][:], flowT[:, HALF * P:STEP * P],
                                 start=True, stop=True).then_inc(hid_done, 1)
                pe.wait_ge(hid_made, s + 1)
                pe.wait_ge(out_made, s)
                nc.tensor.matmul(ps_out[:, 0:STEP * FEAT].rearrange("p (t n) -> p t n", t=STEP), keep["ones3"][:],
                                 keep["bias3"][:, B_NODE:B_NODE + FEAT].unsqueeze(1).to_broadcast([3, STEP, FEAT]),
                                 start=True, stop=False)
                for t in range(STEP):
                    last = nc.tensor.matmul(ps_out[:, t * FEAT:(t + 1) * FEAT], hid[:, t * P:(t + 1) * P],
                                            keep["w_n2"][:], start=False, stop=(t == STEP - 1))
                last.then_inc(out_done, 1)

        @block.scalar
        def _(act):
            with act.Fori(0, steps) as s:
                act.wait_ge(flow_tr, s + 1)
                act.wait_ge(hid_done, s)
                act.activation(flowT[:], ps_flow[:, 0:STEP * P], ACT.Copy).then_inc(flowT_made, 1)
                act.wait_ge(hid_done, s + 1)
                act.wait_ge(out_done, s)
                act.activation(hid[:], ps_hid[:, 0:STEP * P], ACT.Relu, bias=keep["b_n1"][:]).then_inc(hid_made, 1)


_INS = ['x', 'src', 'dst', 'edge_attr_64', 'L0_gnn_Wo1', 'L0_gnn_bo1', 'L0_gnn_Wo2', 'L0_gnn_bo2', 'L0_gnn_Wi1',
        'L0_gnn_bi1', 'L0_gnn_Wi2', 'L0_gnn_bi2', 'L0_gnn_Wn1', 'L0_gnn_bn1', 'L0_gnn_Wn2', 'L0_gnn_bn2']


def kernel(**inputs):
    import numpy as _np
    import concourse.bacc as _bacc
    from concourse import mybir as _mybir
    from concourse.bass_utils import run_bass_kernel_spmd as _run

    nc = _bacc.Bacc("TRN2", target_bir_lowering=False, num_devices=1)
    arrays, args = {}, []
    for name in _INS:
        a = _np.ascontiguousarray(inputs[name])
        arrays[f"in_{name}"] = a
        args.append(nc.dram_tensor(f"in_{name}", a.shape, _mybir.dt.from_np(a.dtype), kind="ExternalInput").ap())
    shape = inputs["x"].shape
    args.append(nc.dram_tensor("out", shape, _mybir.dt.float32, kind="ExternalOutput").ap())
    gnn_kernel(nc, *args)
    r = _run(nc, [arrays], core_ids=[0])
    return r.results[0]["out"]
```

```python
from contextlib import ExitStack

import concourse.bass as bass
from concourse import mybir

P = 128
F32 = mybir.dt.float32
BF16 = mybir.dt.bfloat16
I32 = mybir.dt.int32
U32 = mybir.dt.uint32
U16 = mybir.dt.uint16
ALU = mybir.AluOpType
ACT = mybir.ActivationFunctionType
AX_X = mybir.AxisListType.X

FEAT = 64
HID = 128
TILES = 4
GROUP = TILES * P
WINDOW = 64
EPS = 1e-5

C_SLOT = slice(0, TILES)
C_REL = slice(TILES, 2 * TILES)
C_MASKS = slice(2 * TILES, 4 * TILES)
C_IN = slice(2 * TILES, 4 * TILES, 2)
C_OUT = slice(2 * TILES + 1, 4 * TILES, 2)
C_KEY = slice(4 * TILES, 5 * TILES)
FIELDS = 5 * TILES


class Shapes:

    def __init__(self, n_nodes, n_edges):
        self.nodes, self.edges = n_nodes, n_edges
        self.per_part = -(-n_nodes // P)
        self.padded = self.per_part * P
        self.slots = 2 * self.padded
        self.groups = -(-n_edges // GROUP)
        self.zero_turns = (STEP + 1) * TILES // 2
        self.last_e0 = n_edges - GROUP
        self.repeated = GROUP * self.groups - n_edges
        self.blocks = -(-self.groups // P)
        assert self.repeated % TILES == 0 and (self.repeated // TILES) % 32 == 0
        assert self.groups >= 16 and n_edges >= GROUP and WINDOW <= self.padded


def gnn_kernel(nc, x, src, dst, ea, Wo1, bo1, Wo2, bo2, Wi1, bi1, Wi2, bi2, Wn1, bn1, Wn2, bn2, out):
    sh = Shapes(x.shape[0], src.shape[0])

    proj = nc.dram_tensor("proj", (sh.padded, 2 * HID), F32, kind="Internal").ap()
    row_keys = nc.dram_tensor("row_keys", (sh.blocks * P, 2 * GROUP), U16, kind="Internal").ap()
    bases = nc.dram_tensor("bases", (sh.blocks, P), I32, kind="Internal").ap()
    tables = [nc.dram_tensor(f"flow{t}", (sh.slots + P, FEAT), F32, kind="Internal").ap() for t in range(TILES)]

    with ExitStack() as ctx:
        def sb(name, shape, dt=F32):
            return ctx.enter_context(nc.sbuf_tensor(name, shape, dt))

        keep = {
            "zeros": sb("zeros", [P, 2 * sh.per_part * FEAT // (2 * STEP)]),
            "cols": sb("cols", [P, sh.groups, FIELDS]),
            "ident": sb("ident", [P, P]),
            "tri": sb("tri", [P, P]),
            "pid": sb("pid", [P, 1]),
            "spare": sb("spare", [P, 1]),
            "w_edge": sb("w_edge", [P, HID]),
            "w_second": sb("w_second", [P, 2 * FEAT]),
            "w_n1": sb("w_n1", [P, HID]),
            "w_n2": sb("w_n2", [P, FEAT]),
            "b_n1": sb("b_n1", [P, 1]),
            "ones3": sb("ones3", [3, P], BF16),
            "bias3": sb("bias3", [3, B_END], BF16),
            "base_row": sb("base_row", [1, sh.blocks * P], I32),
            "flag": sb("flag", [1, 1], I32),
        }
        tables_zeroed = [ctx.enter_context(nc.semaphore(f"tables_zeroed{r}")) for r in range(2)]
        x_again = ctx.enter_context(nc.semaphore("x_again"))
        prepare(nc, sh, keep, x, src, dst, Wo1, bo1, Wo2, bo2, Wi1, bi1, Wi2, bi2, Wn1, bn1, Wn2, bn2,
                proj, row_keys, bases, tables, tables_zeroed)
        x_sb = sb("x_kept", [P, sh.per_part, FEAT])
        edge_phase(nc, sh, keep, ea, proj, row_keys, tables, tables_zeroed, x, x_sb, x_again)
        node_phase(nc, sh, keep, x_sb, x_again, tables, out)


B_SECOND = 0
B_NODE = 2 * FEAT
B_END = B_NODE + FEAT

STEP = 7


def run_turns(eng, turns, body, first=1):
    for turn in range(first):
        body(turn)
    with eng.Fori(first, turns - 1) as turn:
        body(turn)
    body(turns - 1)


def load_nodes(eng, sh, x, x_sb, loaded):
    J, full = sh.per_part, P - 1
    tail = sh.nodes - full * J
    for a, b in ((0, 112), (112, full)):
        eng.dma_start(x_sb[a:b, :, :], x[a * J:b * J, :].rearrange("(p j) f -> p j f", j=J)).then_inc(loaded, 16)
    for at, rows in ((0, x[full * J:sh.nodes, :]), (tail, x[0:J - tail, :])):
        eng.dma_start(x_sb[full:P, at:at + rows.shape[0], :],
                      rows.rearrange("(p j) f -> p j f", p=1)).then_inc(loaded, 16)


def prepare(nc, sh, keep, x, src, dst, Wo1, bo1, Wo2, bo2, Wi1, bi1, Wi2, bi2, Wn1, bn1, Wn2, bn2,
            proj, row_keys, bases, tables, tables_zeroed):
    cols, ident, tri, pid, spare = (keep[k] for k in ("cols", "ident", "tri", "pid", "spare"))
    NB, J = sh.blocks, sh.per_part
    steps = J // STEP
    turns = steps // 2
    assert J % (2 * STEP) == 0
    whole = (sh.groups - 1) // P
    odd = sh.groups - 1 - whole * P
    zero_runs = 2 * STEP
    zero_len = sh.slots * FEAT // P // zero_runs
    halves = (slice(0, J // 2), slice(J // 2, J))
    FIRST = 4

    with ExitStack() as ctx:
        def sb(name, shape, dt=F32):
            return ctx.enter_context(nc.sbuf_tensor(name, shape, dt))

        def sem(name):
            return ctx.enter_context(nc.semaphore(name))

        src_i = sb("src_i", [P, NB, GROUP], I32)
        dst_i = sb("dst_i", [P, NB, GROUP], I32)
        slot_r = sb("slot_r", [P, NB, GROUP])
        in_r = sb("in_r", [P, NB, GROUP])
        out_r = sb("out_r", [P, NB, GROUP])
        key_r = src_i[:].bitcast(F32)
        rows_u = dst_i[:].bitcast(U16).rearrange("q b (k e) -> q b k e", k=2)
        dmin = sb("dmin", [P, NB])
        dmax = sb("dmax", [P, NB])
        base2 = sb("base2", [P, NB])
        base_i = sb("base_i", [P, NB], I32)
        wide = sb("wide", [P, NB])
        wide1 = sb("wide1", [P, 1])
        wide_all = sb("wide_all", [1, 1])
        w_node = sb("w_node", [P, 2 * HID])
        b_row = sb("b_row", [1, B_END])
        b_rest = sb("b_rest", [1, B_END])
        b_parts = sb("b_parts", [1, 3, B_END], BF16)
        eps = sb("eps", [P, 1])
        total = sb("total", [P, J])
        var = sb("var", [P, J])
        rstd = sb("rstd", [P, J])
        x_sb = sb("x_sb", [P, J, FEAT])
        squares = slot_r[:].rearrange("q b e -> q (b e)")[:, 0:J // 2 * FEAT].rearrange("p (j f) -> p j f", f=FEAT)
        normed = sb("normed", [P, 2, STEP, FEAT])
        hT = sb("hT", [P, 2, STEP, P])
        proj_sb = sb("proj_sb", [P, 2, STEP, 2 * HID])

        ps_hT = ctx.enter_context(nc.psum_tensor("ps_hT", [P, 2 * 512], F32))
        ps_proj = ctx.enter_context(nc.psum_tensor("ps_proj", [P, 4 * 512], F32))

        weights_in = sem("weights_in")
        x_in = sem("x_in")
        src_in = sem("src_in")
        dst_in = sem("dst_in")
        const_made = sem("const_made")
        zero_made = sem("zero_made")
        chain = sem("chain")
        biases_split = sem("biases_split")
        biases_in = sem("biases_in")
        cleared = sem("cleared")
        centred = sem("centred")
        squared = sem("squared")
        var_made = sem("var_made")
        rooted = sem("rooted")
        rstd_made = sem("rstd_made")
        normed_made = sem("normed_made")
        hT_tr = sem("hT_tr")
        hT_made = sem("hT_made")
        proj_done = sem("proj_done")
        proj_copied = sem("proj_copied")
        proj_stored = [sem(f"proj_stored{r}") for r in range(2)]
        base_made = sem("base_made")
        rows_made = sem("rows_made")
        rows_stored = sem("rows_stored")
        padded = sem("padded")
        b_first_in = sem("b_first_in")
        bases_out = sem("bases_out")
        bases_in = sem("bases_in")
        fields_made = sem("fields_made")
        col_tr = sem("col_tr")
        col_copied = [sem("col_copied_dve"), sem("col_copied_act")]
        flag_tr = sem("flag_tr")

        block = ctx.enter_context(nc.Block())

        N_WEIGHTS = 12
        N_CONST = 6
        zeros = keep["zeros"]

        kinds = (C_SLOT, C_IN, C_OUT, C_KEY)
        column_sets = [(b * len(kinds) + k, b, min(P, sh.groups - b * P), kind)
                       for b in range(NB) for k, kind in enumerate(kinds)]

        def column_psum(n, q):
            return ps_proj[:, 512 * (n % 4):512 * (n % 4) + 512].rearrange("p (t q) -> p q t", t=TILES)[:, 0:q, :]

        @block.sync
        def _(sp):
            load_nodes(sp, sh, x, x_sb, x_in)
            for ids, ids_i, ids_in in ((src, src_i, src_in), (dst, dst_i, dst_in)):
                sp.dma_start(ids_i[:, 0:whole, :],
                             ids[0:whole * P * GROUP].rearrange("(b q e) -> q b e", q=P, e=GROUP)).then_inc(ids_in, 16)
                for at, n, e0 in ((0, odd, whole * P * GROUP), (odd, 1, sh.last_e0), (odd + 1, P - odd - 1, 0)):
                    sp.dma_start(ids_i[at:at + n, whole, :],
                                 ids[e0:e0 + n * GROUP].rearrange("(q e) -> q e", e=GROUP)).then_inc(ids_in, 16)
            sp.wait_ge(zero_made, 1)
            pieces = []
            for table in tables:
                runs = table[0:sh.slots, :].rearrange("(p c r) f -> p c (r f)", p=P, c=zero_runs)
                pieces += [(runs[:, 2 * c:2 * c + 2, :], zeros[:].unsqueeze(1).to_broadcast([P, 2, zero_len]))
                           for c in range(zero_runs // 2)]
                pieces.append((table[sh.slots:sh.slots + P, :], zeros[:, 0:FEAT]))
            assert len(pieces) == 2 * sh.zero_turns

            def clear(n):
                if n >= 2:
                    sp.wait_ge(tables_zeroed[n % 2], 16 * (n // 2))
                sp.dma_start(*pieces[n]).then_inc(tables_zeroed[n % 2], 16)
            early = len(pieces) * 3 // 4
            for n in range(early):
                clear(n)
            with nc.allow_non_contiguous_dma(reason="one base a group, once"):
                sp.wait_ge(base_made, 1)
                sp.dma_start(bases.rearrange("b q -> q b"), base_i[:]).then_inc(bases_out, 16)
            sp.wait_ge(rows_made, 1)
            sp.dma_start(row_keys.rearrange("(b q) k -> q b k", q=P),
                         rows_u.rearrange("q b k e -> q b (k e)")).then_inc(rows_stored, 16)
            sp.wait_ge(bases_out, 16)
            sp.dma_start(keep["base_row"][:], bases.rearrange("(a b) q -> a (b q)", a=1)).then_inc(bases_in, 16)
            for n in range(early, len(pieces)):
                clear(n)
            sp.wait_ge(rows_stored, 16)
            sp.wait_ge(bases_in, 16)

        @block.gpsimd
        def _(pool):
            pool.memset(ident[:], 0.0).then_inc(cleared, 1)
            pool.memset(tri[:], 1.0).then_inc(cleared, 1)
            pool.memset(keep["ones3"][:], 1.0).then_inc(const_made, 1)
            pool.memset(eps[:], EPS).then_inc(const_made, 1)
            pool.iota(pid[:], pattern=[[0, 1]], base=0, channel_multiplier=1,
                      allow_small_or_imprecise_dtypes=True).then_inc(const_made, 1)
            pool.iota(spare[:], pattern=[[0, 1]], base=sh.slots, channel_multiplier=1,
                      allow_small_or_imprecise_dtypes=True).then_inc(const_made, 1)
            pool.wait_ge(cleared, 2)
            pool.affine_select(out=ident[:], in_=ident[:], compare_op=ALU.not_equal, fill=1.0, base=0,
                               pattern=[[-1, P]], channel_multiplier=1).then_inc(const_made, 1)
            pool.affine_select(out=tri[:], in_=tri[:], compare_op=ALU.is_ge, fill=0.0, base=0,
                               pattern=[[1, P]], channel_multiplier=-1).then_inc(const_made, 1)
            pool.memset(zeros[:], 0.0).then_inc(zero_made, 1)
            pool.wait_ge(rstd_made, 1)

            def norm(turn):
                for r in range(2):
                    s = turn * 2 + r
                    nodes = bass.ds(s * STEP, STEP)
                    if not isinstance(turn, int) or turn > 0:
                        pool.wait_ge(hT_tr, s - 1)
                    pool.tensor_tensor(normed[:, r, :, :], x_sb[:, nodes, :],
                                       rstd[:, nodes].unsqueeze(2).to_broadcast([P, STEP, FEAT]),
                                       ALU.mult).then_inc(normed_made, 1)
            run_turns(pool, turns, norm)

        @block.scalar
        def _(act):
            for at, b in ((B_SECOND, bi2), (B_SECOND + FEAT, bo2), (B_NODE, bn2)):
                act.dma_start(b_row[:, at:at + b.shape[0]], b.rearrange("(a n) -> a n", a=1)).then_inc(weights_in, 16)
            for dst_ap, src_ap in (
                (w_node[0:FEAT, 0:HID], Wi1[0:FEAT, :]), (w_node[0:FEAT, HID:2 * HID], Wo1[0:FEAT, :]),
                (keep["w_edge"][0:FEAT, :], Wi1[FEAT:2 * FEAT, :]), (keep["w_edge"][FEAT:P, :], Wo1[FEAT:2 * FEAT, :]),
                (keep["w_second"][:, 0:FEAT], Wi2), (keep["w_second"][:, FEAT:2 * FEAT], Wo2),
                (keep["w_n1"][:], Wn1), (keep["w_n2"][:], Wn2),
                (keep["b_n1"][:], bn1.rearrange("(p a) -> p a", a=1)),
            ):
                act.dma_start(dst_ap, src_ap).then_inc(weights_in, 16)
            act.wait_ge(padded, 1)
            for at, b in ((0, bi1), (HID, bo1)):
                act.dma_start(w_node[FEAT:FEAT + 1, at:at + HID],
                              b.rearrange("(a n) -> a n", a=1)).then_inc(b_first_in, 16)
            for h, nodes in enumerate(halves):
                act.wait_ge(centred, h + 1)
                if h:
                    act.wait_ge(var_made, 1)
                act.activation(squares, x_sb[:, nodes, :], ACT.Square).then_inc(squared, 1)
            act.wait_ge(var_made, 2)
            act.wait_ge(const_made, N_CONST)
            act.activation(rstd[:], var[:], ACT.Sqrt, scale=1.0 / FEAT, bias=eps[:]).then_inc(rooted, 1)

            def relu_nodes(s, r):
                act.wait_ge(hT_tr, s + 1)
                if not isinstance(s, int) or s >= 2:
                    act.wait_ge(proj_done, 2 * s - 2)
                act.activation(hT[0:FEAT, r, :, :].rearrange("p t n -> p (t n)"), ps_hT[0:FEAT, 0:STEP * P],
                               ACT.Relu).then_inc(hT_made, 1)

            def step(s, r, turn):
                for part, tiles in enumerate((slice(0, FIRST), slice(FIRST, STEP))):
                    act.wait_ge(proj_done, 2 * s + part + 1)
                    if part == 0 and (not isinstance(s, int) or s >= 2):
                        act.wait_ge(proj_stored[r], turn * 16)
                    act.activation(proj_sb[:, r, tiles, :].rearrange("p t n -> p (t n)"),
                                   ps_proj[:, tiles.start * 2 * HID:tiles.stop * 2 * HID],
                                   ACT.Copy).then_inc(proj_copied, 1)
                act.wait_ge(proj_copied, 2 * s + 2)
                act.dma_start(proj.rearrange("(p j) n -> p (j n)", j=J)[:, bass.ds(s * (STEP * 2 * HID), STEP * 2 * HID)],
                              proj_sb[:, r, :, :].rearrange("p t n -> p (t n)")).then_inc(proj_stored[r], 16)

            def body(turn):
                for r in range(2):
                    s = turn * 2 + r
                    if not isinstance(s, int) or s + 1 < steps:
                        relu_nodes(s + 1, 1 - r)
                    step(s, r, turn)
            relu_nodes(0, 0)
            run_turns(act, turns, body)
            for n, b, q, kind in column_sets:
                if n % 2:
                    act.wait_ge(col_tr, n + 1)
                    act.activation(cols[:, b * P:b * P + q, kind], column_psum(n, q),
                                   ACT.Copy).then_inc(col_copied[1], 1)
            act.wait_ge(biases_split, 3)
            for k in range(3):
                act.dma_start(keep["bias3"][k:k + 1, :], b_parts[:, k, :]).then_inc(biases_in, 16)
            for r in range(2):
                act.wait_ge(proj_stored[r], 16 * turns)
            act.wait_ge(biases_in, 16 * 3)

        @block.vector
        def _(dve):
            links = [0]

            def link(ins):
                links[0] += 1
                ins.then_inc(chain, 1)
                dve.wait_ge(chain, links[0])

            nc.vector.memset(w_node[FEAT:P, :], 0.0).then_inc(padded, 1)
            link(nc.vector.memset(hT[FEAT:P, :, :, :], 0.0))
            nc.vector.memset(hT[FEAT:FEAT + 1, :, :, :], 1.0).then_inc(padded, 1)

            dve.wait_ge(x_in, 16 * 4)
            for nodes in halves:
                link(nc.vector.tensor_reduce(total[:, nodes], x_sb[:, nodes, :], AX_X, ALU.add))
                nc.vector.scalar_tensor_tensor(x_sb[:, nodes, :],
                                               total[:, nodes].unsqueeze(2).to_broadcast([P, J // 2, FEAT]),
                                               -1.0 / FEAT, x_sb[:, nodes, :], ALU.mult, ALU.add).then_inc(centred, 1)
            for h, nodes in enumerate(halves):
                dve.wait_ge(squared, h + 1)
                nc.vector.tensor_reduce(var[:, nodes], squares, AX_X, ALU.add).then_inc(var_made, 1)

            dve.wait_ge(src_in, 16 * 4)
            dve.wait_ge(dst_in, 16 * 4)
            nc.vector.tensor_tensor(out_r[:], src_i[:], dst_i[:], ALU.is_lt)
            link(nc.vector.tensor_tensor(in_r[:], src_i[:], dst_i[:], ALU.is_gt))
            dve.wait_ge(rooted, 1)
            nc.vector.reciprocal(rstd[:], rstd[:]).then_inc(rstd_made, 1)
            dve.wait_ge(var_made, 2)
            link(nc.vector.scalar_tensor_tensor(slot_r[:], src_i[:], 2.0, out_r[:], ALU.mult, ALU.add))
            link(nc.vector.scalar_tensor_tensor(key_r, dst_i[:], 2.0, out_r[:], ALU.mult, ALU.add))
            nc.vector.tensor_reduce(dmin[:], dst_i[:], AX_X, ALU.min)
            link(nc.vector.tensor_reduce(dmax[:], dst_i[:], AX_X, ALU.max))
            link(nc.vector.tensor_scalar(dmin[:], dmin[:], float(sh.padded - WINDOW), None, ALU.min))
            nc.vector.tensor_copy(base_i[:], dmin[:]).then_inc(base_made, 1)
            nc.vector.tensor_scalar(base2[:], dmin[:], 2.0, None, ALU.mult)
            link(nc.vector.tensor_tensor(wide[:], dmax[:], dmin[:], ALU.subtract))
            nc.vector.tensor_reduce(wide1[:], wide[:], AX_X, ALU.max).then_inc(fields_made, 1)
            for b in range(NB):
                nc.vector.tensor_copy(rows_u[:, b, 0, :].rearrange("q (t p) -> q p t", t=TILES),
                                      slot_r[:, b, :].rearrange("q (p t) -> q p t", t=TILES))
                last = nc.vector.tensor_scalar(rows_u[:, b, 1, :].rearrange("q (t p) -> q p t", t=TILES),
                                               key_r[:, b, :].rearrange("q (p t) -> q p t", t=TILES),
                                               base2[:, b:b + 1], None, ALU.subtract)
            last.then_inc(rows_made, 1)

            dve.wait_ge(weights_in, 16 * N_WEIGHTS)
            nc.vector.tensor_copy(b_parts[:, 0, :], b_row[:]).then_inc(biases_split, 1)
            dve.wait_ge(biases_split, 1)
            link(nc.vector.tensor_tensor(b_rest[:], b_row[:], b_parts[:, 0, :], ALU.subtract))
            nc.vector.tensor_copy(b_parts[:, 1, :], b_rest[:]).then_inc(biases_split, 1)
            dve.wait_ge(biases_split, 2)
            link(nc.vector.tensor_tensor(b_rest[:], b_rest[:], b_parts[:, 1, :], ALU.subtract))
            nc.vector.tensor_copy(b_parts[:, 2, :], b_rest[:]).then_inc(biases_split, 1)

            for n, b, q, kind in column_sets:
                if n % 2 == 0:
                    dve.wait_ge(col_tr, n + 1)
                    if kind == C_SLOT:
                        nc.vector.tensor_scalar(cols[:, b * P:b * P + q, C_REL], column_psum(n, q), spare[:, 0:1], None,
                                                ALU.subtract)
                    nc.vector.tensor_copy(cols[:, b * P:b * P + q, kind], column_psum(n, q)).then_inc(col_copied[0], 1)
            dve.wait_ge(flag_tr, 1)
            link(nc.vector.tensor_reduce(wide_all[:], ps_hT[0:1, 0:P], AX_X, ALU.max))
            nc.vector.tensor_scalar(keep["flag"][:], wide_all[:], float(WINDOW - 1), None, ALU.is_gt)
            for copied in col_copied:
                dve.wait_ge(copied, len(column_sets) // 2)
            nc.vector.memset(cols[0:sh.repeated // TILES, sh.groups - 1, C_MASKS], 0.0)

        @block.tensor
        def _(pe):
            held = pe.alloc_register("held")
            pe.wait_ge(const_made, N_CONST)
            pe.wait_ge(weights_in, 16 * N_WEIGHTS)
            pe.wait_ge(padded, 2)
            pe.wait_ge(b_first_in, 16 * 2)

            def turn_over(s, r):
                due, copied = s + 1, s
                if not isinstance(s, int):
                    pe.reg_mov(held, due)
                    pe.reg_mov(held, copied)
                pe.wait_ge(normed_made, 1)
                pe.wait_ge(normed_made, due)
                if not isinstance(s, int) or s >= 1:
                    pe.wait_ge(hT_made, copied)
                for t in range(STEP):
                    last = nc.tensor.transpose(ps_hT[0:FEAT, t * P:(t + 1) * P], normed[:, r, t, :], ident[:])
                last.then_inc(hT_tr, 1)

            def project(s, r):
                pe.wait_ge(hT_made, s + 1)
                for part, tiles in enumerate((range(0, FIRST), range(FIRST, STEP))):
                    if not isinstance(s, int) or s >= 1:
                        pe.wait_ge(proj_copied, 2 * s - 1 + part)
                    for t in tiles:
                        o = ps_proj[:, t * 2 * HID:(t + 1) * 2 * HID]
                        last = nc.tensor.matmul(o, hT[:, r, t, :], w_node[:], start=True, stop=True)
                    last.then_inc(proj_done, 1)

            def body(turn):
                for r in range(2):
                    s = turn * 2 + r
                    if not isinstance(s, int) or s + 1 < steps:
                        turn_over(s + 1, 1 - r)
                    project(s, r)
            turn_over(0, 0)
            run_turns(pe, turns, body)
            pe.wait_ge(fields_made, 1)
            nc.tensor.transpose(ps_hT[0:1, 0:P], wide1[:], ident[:]).then_inc(flag_tr, 1)
            pe.wait_ge(proj_copied, 2 * steps)
            fields = (slot_r[:], in_r[:], out_r[:], key_r)
            for n, b, q, kind in column_sets:
                if n >= 4:
                    pe.wait_ge(col_copied[n % 2], (n - 4) // 2 + 1)
                for t in range(TILES):
                    last = nc.tensor.transpose(ps_proj[:, 512 * (n % 4) + t * P:512 * (n % 4) + (t + 1) * P],
                                               fields[n % 4][:, b, :].rearrange("q (p t) -> q t p", t=TILES)[:, t, :],
                                               ident[:])
                last.then_inc(col_tr, 1)


class Group:

    def __init__(self, it, s):
        self.n = it * 4 + s
        self.ring4, self.ring2 = s % 4, s % 2
        self.turn = it + s // 4


def run_steps(eng, groups, lag, step):
    turns = groups // 4
    for i in range(8):
        step(0, i)
    with eng.Fori(2, turns) as it:
        for s in range(4):
            step(it, s)
    for s in range(groups + lag - 4 * turns):
        step(turns, s)


def edge_phase(nc, sh, keep, ea, proj, row_keys, tables, tables_zeroed, x, x_sb, x_again):
    cols, ident, tri, pid, spare = (keep[k] for k in ("cols", "ident", "tri", "pid", "spare"))
    G = sh.groups
    LAG = 3

    with ExitStack() as ctx:
        def sb(name, shape, dt=F32):
            return ctx.enter_context(nc.sbuf_tensor(name, shape, dt))

        def ps(name, shape):
            return ctx.enter_context(nc.psum_tensor(name, shape, F32))

        def sem(name):
            return ctx.enter_context(nc.semaphore(name))

        edges_sb = sb("edges_sb", [P, 4, TILES, FEAT])
        keys_sb = sb("keys_sb", [P, 4, 2, GROUP], U16)
        window = sb("window", [P, 4, HID])
        col = sb("col", [P, 4, FIELDS])
        masked = sb("masked", [P, 2, TILES, 2, FEAT])
        onehot = sb("onehot", [P, 2, GROUP])
        same = sb("same", [P, 4, TILES, P])
        later = sb("later", [P, 4, TILES])
        kept = sb("kept", [P, 2, TILES])
        slot_u = sb("slot_u", [P, 4, TILES], U32)
        key_u = sb("key_u", [P, 2, TILES], U32)
        picked = sb("picked", [P, 2, TILES, HID])
        maskedT = sb("maskedT", [P, 2, GROUP])
        hidden = sb("hidden", [P, 2, GROUP])
        both = sb("both", [P, 2, TILES, 2, FEAT])
        message = sb("message", [P, 2, TILES, FEAT])
        flow_sb = sb("flow_sb", [P, 4, TILES, FEAT])

        ps_t = ps("ps_t", [P, 2, 512])
        ps_h = ps("ps_h", [P, 2, 512])
        ps_z = ps("ps_z", [P, 2, 512])
        ps_f = ps("ps_f", [P, 2, 512])

        edges_in = [sem(f"edges_in{r}") for r in range(4)]
        keys_in = [sem(f"keys_in{r}") for r in range(4)]
        window_in = [sem(f"window_in{r}") for r in range(4)]
        picked_in = [sem(f"picked_in{r}") for r in range(2)]
        added = [sem(f"added{t}") for t in range(TILES)]
        col_made = sem("col_made")
        masked_made = sem("masked_made")
        onehot_made = sem("onehot_made")
        key_made = sem("key_made")
        same_made = sem("same_made")
        kept_made = sem("kept_made")
        slot_made = sem("slot_made")
        both_made = sem("both_made")
        message_made = sem("message_made")
        transposed = sem("transposed")
        maskedT_made = sem("maskedT_made")
        first_done = sem("first_done")
        hidden_made = sem("hidden_made")
        second_done = sem("second_done")
        summed = sem("summed")
        flow_made = sem("flow_made")

        block = ctx.enter_context(nc.Block())

        def each_path(eng, program):
            with eng.register("wide_flag") as flag:
                eng.reg_load(flag, keep["flag"][0:1, 0:1])
                with eng.If_eq(flag, 0):
                    program(False)
                with eng.Else():
                    program(True)

        @block.sync
        def _(sp):
            def program(general):
                def load(it, s):
                    g = Group(it, s)
                    i = g.n
                    static = isinstance(i, int)
                    r = g.ring4
                    e0 = min(i * GROUP, sh.last_e0) if static else i * GROUP
                    if not static or i >= 4:
                        sp.wait_ge(masked_made, i - 3)
                    sp.dma_start(edges_sb[:, r, :, :].rearrange("p t f -> p (t f)"),
                                 ea[bass.ds(e0, GROUP), :].rearrange("(p t) f -> p (t f)", t=TILES)
                                 ).then_inc(edges_in[r], 16)
                    if not static or i >= 4:
                        sp.wait_ge(same_made, i - 3)
                        if not general:
                            sp.wait_ge(onehot_made, i - 3)
                    sp.dma_start(keys_sb[:, r, :, :].rearrange("p k e -> p (k e)"),
                                 row_keys[bass.ds(i, 1), :].to_broadcast([P, 2 * GROUP])).then_inc(keys_in[r], 16)
                    if not general:
                        base = sp.value_load(keep["base_row"][0:1, bass.ds(i, 1)], min_val=0,
                                             max_val=sh.padded - WINDOW)
                        if not static or i >= 4:
                            sp.wait_ge(first_done, i - 3)
                        sp.dma_start(window[:, r, :],
                                     proj[bass.ds(base, WINDOW), :].rearrange("n (d h) -> (n d) h", d=2)
                                     ).then_inc(window_in[r], 16)
                run_steps(sp, G, 0, load)
            each_path(sp, program)
            load_nodes(sp, sh, x, x_sb, x_again)

        @block.vector
        def _(dve):
            def program(general):
                def step(it, s):
                    g, d = Group(it, s), Group(it, s - LAG)
                    i, j = g.n, d.n
                    static = isinstance(i, int)
                    front, back = not static or i < G, not static or 0 <= j < G
                    old = not static or i >= 4
                    r = g.ring4
                    if front:
                        if old:
                            dve.wait_ge(kept_made, i - 3)
                        nc.vector.tensor_copy(col[:, r, :],
                                              cols[:, bass.ds(i, 1), :].rearrange("p a k -> p (a k)")
                                              ).then_inc(col_made, 1)
                    if back:
                        dve.wait_ge(second_done, j + 1)
                        if not static or j >= 2:
                            dve.wait_ge(message_made, j - 1)
                        nc.vector.scalar_tensor_tensor(
                            both[:, d.ring2, :, :, :].rearrange("p t d f -> p (t d) f"),
                            ps_z[:, d.ring2, :].rearrange("p (m f) -> p m f", f=FEAT), 0.0,
                            col[:, d.ring4, C_MASKS].unsqueeze(2).to_broadcast([P, 2 * TILES, FEAT]),
                            ALU.max, ALU.mult).then_inc(both_made, 1)
                    if front:
                        dve.wait_ge(col_made, i + 1)
                        dve.wait_ge(edges_in[r], 16 * (g.turn + 1))
                        if old or i >= 2:
                            dve.wait_ge(transposed, i - 1)
                        nc.vector.tensor_tensor(
                            masked[:, g.ring2, :, :, :],
                            edges_sb[:, r, :, :].unsqueeze(2).to_broadcast([P, TILES, 2, FEAT]),
                            col[:, r, C_MASKS].rearrange("p (t d) -> p t d", d=2).unsqueeze(3)
                            .to_broadcast([P, TILES, 2, FEAT]), ALU.mult).then_inc(masked_made, 1)
                        dve.wait_ge(keys_in[r], 16 * (g.turn + 1))
                        if old:
                            dve.wait_ge(summed, i - 3)
                        for t in range(TILES):
                            last = nc.vector.scalar_tensor_tensor(
                                same[:, r, t, :], keys_sb[:, r, 0, t * P:(t + 1) * P], col[:, r, t:t + 1],
                                tri[:], ALU.is_equal, ALU.mult, accum_out=later[:, r, t:t + 1])
                        last.then_inc(same_made, 1)
                    if back:
                        dve.wait_ge(both_made, j + 1)
                        if not static or j >= 2:
                            dve.wait_ge(summed, j - 1)
                        nc.vector.tensor_tensor(message[:, d.ring2, :, :], both[:, d.ring2, :, 0, :],
                                                both[:, d.ring2, :, 1, :], ALU.add).then_inc(message_made, 1)
                        dve.wait_ge(same_made, j + 1)
                        if not static or j >= 2:
                            dve.wait_ge(slot_made, j - 1)
                        nc.vector.scalar_tensor_tensor(
                            kept[:, d.ring2, :], later[:, d.ring4, :], 1.0, col[:, d.ring4, C_REL],
                            ALU.is_equal, ALU.mult).then_inc(kept_made, 1)
                    if front:
                        if general:
                            if not static or i >= 2:
                                for_ring = 16 * TILES
                                dve.wait_ge(picked_in[g.ring2], for_ring * (i // 2) if static else for_ring * (it * 2 + s // 2))
                            nc.vector.tensor_copy(key_u[:, g.ring2, :], col[:, r, C_KEY]).then_inc(key_made, 1)
                        else:
                            if not static or i >= 2:
                                dve.wait_ge(first_done, i - 1)
                            nc.vector.tensor_scalar(onehot[:, g.ring2, :], keys_sb[:, r, 1, :], pid[:, 0:1], None,
                                                    ALU.is_equal).then_inc(onehot_made, 1)
                    if back:
                        dve.wait_ge(kept_made, j + 1)
                        if not static or j >= 4:
                            for t in range(TILES):
                                dve.wait_ge(added[t], 16 * (j - 3))
                        nc.vector.tensor_scalar(slot_u[:, d.ring4, :], kept[:, d.ring2, :], spare[:, 0:1], None,
                                                ALU.add).then_inc(slot_made, 1)
                run_steps(dve, G, LAG, step)
            each_path(dve, program)

        @block.tensor
        def _(pe):
            def program(general):
                def step(it, s):
                    a, b, c, d = (Group(it, s - k) for k in range(4))
                    static = isinstance(a.n, int)

                    def on(g):
                        return not static or 0 <= g.n < G
                    if on(a):
                        pe.wait_ge(masked_made, a.n + 1)
                        if not static or a.n >= 2:
                            pe.wait_ge(maskedT_made, a.n - 1)
                        for t in range(TILES):
                            last = nc.tensor.transpose(
                                ps_t[:, a.ring2, t * P:(t + 1) * P],
                                masked[:, a.ring2, t, :, :].rearrange("p d f -> p (d f)"), ident[:])
                        last.then_inc(transposed, 1)
                    if on(c):
                        pe.wait_ge(hidden_made, c.n + 1)
                        if not static or c.n >= 2:
                            pe.wait_ge(both_made, c.n - 1)
                        nc.tensor.matmul(
                            ps_z[:, c.ring2, :].rearrange("p (t n) -> p t n", t=TILES), keep["ones3"][:],
                            keep["bias3"][:, B_SECOND:B_SECOND + 2 * FEAT].unsqueeze(1).to_broadcast([3, TILES, 2 * FEAT]),
                            start=True, stop=False)
                        for t in range(TILES):
                            last = nc.tensor.matmul(
                                ps_z[:, c.ring2, t * P:(t + 1) * P], hidden[:, c.ring2, t * P:(t + 1) * P],
                                keep["w_second"][:], start=False, stop=(t == TILES - 1))
                        last.then_inc(second_done, 1)
                    if on(b):
                        pe.wait_ge(maskedT_made, b.n + 1)
                        if not static or b.n >= 2:
                            pe.wait_ge(hidden_made, b.n - 1)
                        nc.tensor.matmul(ps_h[:, b.ring2, :], keep["w_edge"][:], maskedT[:, b.ring2, :],
                                         start=True, stop=False)
                        if general:
                            rounds = b.n // 2 if static else it * 2 + (s - 1) // 2
                            pe.wait_ge(picked_in[b.ring2], 16 * TILES * (rounds + 1))
                            for t in range(TILES):
                                last = nc.tensor.matmul(ps_h[:, b.ring2, t * P:(t + 1) * P],
                                                        picked[:, b.ring2, t, :], ident[:],
                                                        start=False, stop=(t == TILES - 1))
                        else:
                            pe.wait_ge(window_in[b.ring4], 16 * (b.turn + 1))
                            pe.wait_ge(onehot_made, b.n + 1)
                            last = nc.tensor.matmul(ps_h[:, b.ring2, :], window[:, b.ring4, :],
                                                    onehot[:, b.ring2, :], start=False, stop=True)
                        last.then_inc(first_done, 1)
                    if on(d):
                        pe.wait_ge(message_made, d.n + 1)
                        pe.wait_ge(same_made, d.n + 1)
                        if not static or d.n >= 2:
                            pe.wait_ge(flow_made, d.n - 1)
                        for t in range(TILES):
                            last = nc.tensor.matmul(ps_f[:, d.ring2, t * FEAT:(t + 1) * FEAT], same[:, d.ring4, t, :],
                                                    message[:, d.ring2, t, :], start=True, stop=True)
                        last.then_inc(summed, 1)
                run_steps(pe, G, LAG, step)
            each_path(pe, program)

        @block.scalar
        def _(act):
            def program(general):
                def step(it, s):
                    a, b, d = Group(it, s), Group(it, s - 1), Group(it, s - 3)
                    static = isinstance(a.n, int)

                    def on(g):
                        return not static or 0 <= g.n < G
                    if on(a):
                        act.wait_ge(transposed, a.n + 1)
                        if not static or a.n >= 2:
                            act.wait_ge(first_done, a.n - 1)
                        act.activation(maskedT[:, a.ring2, :], ps_t[:, a.ring2, :], ACT.Copy).then_inc(maskedT_made, 1)
                    if on(b):
                        act.wait_ge(first_done, b.n + 1)
                        if not static or b.n >= 2:
                            act.wait_ge(second_done, b.n - 1)
                        act.activation(hidden[:, b.ring2, :], ps_h[:, b.ring2, :], ACT.Relu).then_inc(hidden_made, 1)
                    if on(d):
                        act.wait_ge(summed, d.n + 1)
                        if not static or d.n >= 4:
                            for t in range(TILES):
                                act.wait_ge(added[t], 16 * (d.n - 3))
                        act.activation(flow_sb[:, d.ring4, :, :].rearrange("p t f -> p (t f)"),
                                       ps_f[:, d.ring2, 0:TILES * FEAT], ACT.Copy).then_inc(flow_made, 1)
                run_steps(act, G, LAG, step)
            each_path(act, program)

        @block.gpsimd
        def _(pool):
            held = pool.alloc_register("held")

            def value(v):
                if not isinstance(v, int):
                    pool.reg_mov(held, v)
                return v

            def program(general):
                def step(it, s):
                    g, d = Group(it, s), Group(it, s - LAG)
                    static = isinstance(g.n, int)
                    if general and (not static or g.n < G):
                        keys_due, free_due = value(g.n + 1), value(g.n - 1)
                        pool.wait_ge(key_made, 1)
                        pool.wait_ge(key_made, keys_due)
                        if not static or g.n >= 2:
                            pool.wait_ge(first_done, free_due)
                        for t in range(TILES):
                            pool.indirect_dma_start(
                                out=picked[:, g.ring2, t, :], out_offset=None,
                                in_=proj.rearrange("n (d h) -> (n d) h", d=2),
                                in_offset=bass.IndirectOffsetOnAxis(ap=key_u[:, g.ring2, t:t + 1], axis=0),
                            ).then_inc(picked_in[g.ring2], 16)
                    if not static or 0 <= d.n < G:
                        due, added_due = value(d.n + 1), value(16 * d.n)
                        pool.wait_ge(flow_made, 1)
                        pool.wait_ge(flow_made, due)
                        pool.wait_ge(slot_made, due)
                        for t in range(TILES):
                            if not static or d.n >= 1:
                                if t:
                                    pool.wait_ge(flow_made, 1)
                                pool.wait_ge(added[t], added_due)
                            pool.indirect_dma_start(
                                out=tables[t],
                                out_offset=bass.IndirectOffsetOnAxis(ap=slot_u[:, d.ring4, t:t + 1], axis=0),
                                in_=flow_sb[:, d.ring4, t, :], in_offset=None, compute_op=ALU.add,
                            ).then_inc(added[t], 16)
                run_steps(pool, G, LAG, step)
            for zeroed in tables_zeroed:
                pool.wait_ge(zeroed, 16 * sh.zero_turns)
            each_path(pool, program)
            for t in range(TILES):
                pool.wait_ge(added[t], 16 * G)


def node_phase(nc, sh, keep, x_sb, x_again, tables, out):
    ident = keep["ident"]
    J = sh.per_part
    steps = J // STEP
    turns = steps // 2
    LOT = STEP * 2 * FEAT
    full = P - 1
    tail = sh.nodes - full * J
    pieces = [(0, (steps // 2) * STEP, steps // 2), ((steps // 2) * STEP, (steps - 1) * STEP, steps - 1),
              ((steps - 1) * STEP, J, steps)]

    with ExitStack() as ctx:
        def sb(name, shape, dt=F32):
            return ctx.enter_context(nc.sbuf_tensor(name, shape, dt))

        def ps(name, shape):
            return ctx.enter_context(nc.psum_tensor(name, shape, F32))

        def sem(name):
            return ctx.enter_context(nc.semaphore(name))

        parts = sb("parts", [P, 2, TILES, LOT])
        pairs = sb("pairs", [P, 2, 2, LOT])
        flow = sb("flow", [P, 2, STEP, 2 * FEAT])
        flowT = sb("flowT", [P, 2, STEP * P])
        hid = sb("hid", [P, 2, STEP * P])
        outs = sb("outs", [P, J, FEAT])

        ps_flow = ps("ps_flow", [P, 2 * 512])
        ps_hid = ps("ps_hid", [P, 2 * 512])
        ps_out = ps("ps_out", [P, 2, 512])

        parts_in = [sem(f"parts_in{r}") for r in range(2)]
        front_made = sem("front_made")
        back_made = sem("back_made")
        flow_added = sem("flow_added")
        flow_tr = sem("flow_tr")
        flowT_made = sem("flowT_made")
        hid_done = sem("hid_done")
        hid_made = sem("hid_made")
        out_done = sem("out_done")
        out_made = sem("out_made")
        out_stored = sem("out_stored")

        block = ctx.enter_context(nc.Block())
        flat = [t[0:sh.slots, :].rearrange("(p j) f -> p (j f)", p=P) for t in tables]

        def lagged(eng, lag, step):
            def body(turn):
                for r in range(2):
                    step(turn * 2 + r, r, turn)
            run_turns(eng, turns, body, first=2)
            for s in range(steps, steps + lag):
                step(s, s % 2, s // 2)

        @block.sync
        def _(sp):
            def load(s, r, turn):
                if not isinstance(s, int) or s >= 2:
                    sp.wait_ge(front_made, s - 1)
                    sp.wait_ge(back_made, s - 1)
                for t in range(TILES):
                    sp.dma_start(parts[:, r, t, :], flat[t][:, bass.ds(s * LOT, LOT)]).then_inc(parts_in[r], 16)
            lagged(sp, 0, load)

        @block.gpsimd
        def _(pool):
            def back(s, r, turn):
                pool.wait_ge(parts_in[r], (turn + 1) * (16 * TILES))
                if not isinstance(s, int) or s >= 2:
                    pool.wait_ge(flow_added, s - 1)
                pool.tensor_tensor(pairs[:, r, 1, :], parts[:, r, 2, :], parts[:, r, 3, :],
                                   ALU.add).then_inc(back_made, 1)
            lagged(pool, 0, back)

        @block.vector
        def _(dve):
            dve.wait_ge(x_again, 16 * 4)

            def step(s, r, turn):
                static = isinstance(s, int)
                if not static or s < steps:
                    dve.wait_ge(parts_in[r], (turn + 1) * (16 * TILES))
                    if not static or s >= 2:
                        dve.wait_ge(flow_added, s - 1)
                    nc.vector.tensor_tensor(pairs[:, r, 0, :], parts[:, r, 0, :], parts[:, r, 1, :],
                                            ALU.add).then_inc(front_made, 1)
                if not static or s >= 3:
                    j = s - 3
                    dve.wait_ge(out_done, s - 2)
                    nc.vector.scalar_tensor_tensor(
                        outs[:, bass.ds(j * STEP, STEP), :],
                        ps_out[:, 1 - r, 0:STEP * FEAT].rearrange("p (t f) -> p t f", f=FEAT),
                        0.0, x_sb[:, bass.ds(j * STEP, STEP), :], ALU.max, ALU.add).then_inc(out_made, 1)
                if not static or s < steps:
                    dve.wait_ge(front_made, s + 1)
                    dve.wait_ge(back_made, s + 1)
                    if not static or s >= 2:
                        dve.wait_ge(flow_tr, s - 1)
                    nc.vector.tensor_tensor(flow[:, r, :, :].rearrange("p t n -> p (t n)"), pairs[:, r, 0, :],
                                            pairs[:, r, 1, :], ALU.add).then_inc(flow_added, 1)
            lagged(dve, 3, step)

        @block.tensor
        def _(pe):
            def step(s, r, turn):
                static = isinstance(s, int)
                if not static or s < steps:
                    pe.wait_ge(flow_added, s + 1)
                    if not static or s >= 1:
                        pe.wait_ge(flowT_made, s)
                    for t in range(STEP):
                        last = nc.tensor.transpose(ps_flow[:, t * P:(t + 1) * P], flow[:, r, t, :], ident[:])
                    last.then_inc(flow_tr, 1)
                if not static or 1 <= s <= steps:
                    pe.wait_ge(flowT_made, s)
                    if not static or s >= 2:
                        pe.wait_ge(hid_made, s - 1)
                    for a, b in ((0, 512), (512, STEP * P)):
                        last = nc.tensor.matmul(ps_hid[:, a:b], keep["w_n1"][:], flowT[:, 1 - r, a:b],
                                                start=True, stop=True)
                    last.then_inc(hid_done, 1)
                if not static or s >= 2:
                    pe.wait_ge(hid_made, s - 1)
                    if not static or s >= 4:
                        pe.wait_ge(out_made, s - 3)
                    nc.tensor.matmul(ps_out[:, r, 0:STEP * FEAT].rearrange("p (t n) -> p t n", t=STEP),
                                     keep["ones3"][:],
                                     keep["bias3"][:, B_NODE:B_NODE + FEAT].unsqueeze(1).to_broadcast([3, STEP, FEAT]),
                                     start=True, stop=False)
                    for t in range(STEP):
                        last = nc.tensor.matmul(ps_out[:, r, t * FEAT:(t + 1) * FEAT], hid[:, r, t * P:(t + 1) * P],
                                                keep["w_n2"][:], start=False, stop=(t == STEP - 1))
                    last.then_inc(out_done, 1)
            lagged(pe, 2, step)

        @block.scalar
        def _(act):
            sent = [0]

            def store(piece):
                a, b, after = piece
                act.wait_ge(out_made, after)
                whole = out[0:full * J, :].rearrange("(p j) f -> p j f", j=J)
                for p0, p1 in ((0, 112), (112, full)):
                    act.dma_start(whole[p0:p1, a:b, :], outs[p0:p1, a:b, :]).then_inc(out_stored, 16)
                    sent[0] += 1
                if a < tail:
                    b = min(b, tail)
                    act.dma_start(out[full * J + a:full * J + b, :].rearrange("(p j) f -> p j f", p=1),
                                  outs[full:P, a:b, :]).then_inc(out_stored, 16)
                    sent[0] += 1

            def step(s, r, turn):
                static = isinstance(s, int)
                if not static or s < steps:
                    act.wait_ge(flow_tr, s + 1)
                    if not static or s >= 2:
                        act.wait_ge(hid_done, s - 1)
                    act.activation(flowT[:, r, :], ps_flow[:, 0:STEP * P], ACT.Copy).then_inc(flowT_made, 1)
                if not static or 1 <= s <= steps:
                    act.wait_ge(hid_done, s)
                    if not static or s >= 3:
                        act.wait_ge(out_done, s - 2)
                    act.activation(hid[:, 1 - r, :], ps_hid[:, 0:STEP * P], ACT.Relu,
                                   bias=keep["b_n1"][:]).then_inc(hid_made, 1)
            lagged(act, 1, step)
            for piece in pieces:
                store(piece)
            act.wait_ge(out_stored, 16 * sent[0])


_INS = ['x', 'src', 'dst', 'edge_attr_64', 'L0_gnn_Wo1', 'L0_gnn_bo1', 'L0_gnn_Wo2', 'L0_gnn_bo2', 'L0_gnn_Wi1',
        'L0_gnn_bi1', 'L0_gnn_Wi2', 'L0_gnn_bi2', 'L0_gnn_Wn1', 'L0_gnn_bn1', 'L0_gnn_Wn2', 'L0_gnn_bn2']


def kernel(**inputs):
    import numpy as _np
    import concourse.bacc as _bacc
    from concourse import mybir as _mybir
    from concourse.bass_utils import run_bass_kernel_spmd as _run

    nc = _bacc.Bacc("TRN2", target_bir_lowering=False, num_devices=1)
    arrays, args = {}, []
    for name in _INS:
        a = _np.ascontiguousarray(inputs[name])
        arrays[f"in_{name}"] = a
        args.append(nc.dram_tensor(f"in_{name}", a.shape, _mybir.dt.from_np(a.dtype), kind="ExternalInput").ap())
    shape = inputs["x"].shape
    args.append(nc.dram_tensor("out", shape, _mybir.dt.float32, kind="ExternalOutput").ap())
    gnn_kernel(nc, *args)
    r = _run(nc, [arrays], core_ids=[0])
    return r.results[0]["out"]
```

```python
from contextlib import ExitStack

import concourse.bass as bass
from concourse import mybir

P = 128
F32 = mybir.dt.float32
BF16 = mybir.dt.bfloat16
I32 = mybir.dt.int32
U32 = mybir.dt.uint32
U16 = mybir.dt.uint16
ALU = mybir.AluOpType
ACT = mybir.ActivationFunctionType
AX_X = mybir.AxisListType.X

FEAT = 64
HID = 128
TILES = 4
GROUP = TILES * P
WINDOW = 64
EPS = 1e-5
EARLY = 36
LATE = 12
CLEARING = 3

C_SLOT = slice(0, TILES)
C_REL = slice(TILES, 2 * TILES)
C_MASKS = slice(2 * TILES, 4 * TILES)
C_IN = slice(2 * TILES, 4 * TILES, 2)
C_OUT = slice(2 * TILES + 1, 4 * TILES, 2)
C_KEY = slice(4 * TILES, 5 * TILES)
FIELDS = 5 * TILES


class Shapes:

    def __init__(self, n_nodes, n_edges):
        self.nodes, self.edges = n_nodes, n_edges
        self.per_part = -(-n_nodes // P)
        self.padded = self.per_part * P
        self.slots = 2 * self.padded
        self.groups = -(-n_edges // GROUP)
        self.last_e0 = n_edges - GROUP
        self.repeated = GROUP * self.groups - n_edges
        self.blocks = -(-self.groups // P)
        assert self.repeated % TILES == 0 and (self.repeated // TILES) % 32 == 0
        assert self.groups >= 16 and n_edges >= GROUP and WINDOW <= self.padded


def gnn_kernel(nc, x, src, dst, ea, Wo1, bo1, Wo2, bo2, Wi1, bi1, Wi2, bi2, Wn1, bn1, Wn2, bn2, out):
    sh = Shapes(x.shape[0], src.shape[0])

    proj = nc.dram_tensor("proj", (sh.padded, 2 * HID), F32, kind="Internal").ap()
    row_keys = nc.dram_tensor("row_keys", (sh.blocks * P, 2 * GROUP), U16, kind="Internal").ap()
    bases = nc.dram_tensor("bases", (sh.blocks, P), I32, kind="Internal").ap()
    tables = [nc.dram_tensor(f"flow{t}", (sh.slots + P, FEAT), F32, kind="Internal").ap() for t in range(TILES)]

    with ExitStack() as ctx:
        def sb(name, shape, dt=F32):
            return ctx.enter_context(nc.sbuf_tensor(name, shape, dt))

        keep = {
            "zeros": sb("zeros", [P, 2 * sh.per_part * FEAT // (2 * STEP)]),
            "cols": sb("cols", [P, sh.groups, FIELDS]),
            "ident": sb("ident", [P, P]),
            "tri": sb("tri", [P, P]),
            "pid": sb("pid", [P, 1]),
            "spare": sb("spare", [P, 1]),
            "w_edge": sb("w_edge", [P, HID]),
            "w_second": sb("w_second", [P, 2 * FEAT]),
            "w_n1": sb("w_n1", [P, HID]),
            "w_n2": sb("w_n2", [P, FEAT]),
            "b_n1": sb("b_n1", [P, 1]),
            "ones3": sb("ones3", [3, P], BF16),
            "bias3": sb("bias3", [3, B_END], BF16),
            "base_row": sb("base_row", [1, sh.blocks * P], I32),
            "flag": sb("flag", [1, 1], I32),
        }
        tables_zeroed = [ctx.enter_context(nc.semaphore(f"tables_zeroed{r}")) for r in range(CLEARING)]
        late_zeroed = [ctx.enter_context(nc.semaphore(f"late_zeroed{r}")) for r in range(CLEARING)]
        x_again = ctx.enter_context(nc.semaphore("x_again"))
        pieces = table_pieces(sh, tables)
        prepare(nc, sh, keep, x, src, dst, Wo1, bo1, Wo2, bo2, Wi1, bi1, Wi2, bi2, Wn1, bn1, Wn2, bn2,
                proj, row_keys, bases, pieces[:-LATE], tables_zeroed)
        x_sb = sb("x_kept", [P, sh.per_part, FEAT])
        edge_phase(nc, sh, keep, ea, proj, row_keys, tables, pieces[-LATE:], tables_zeroed, late_zeroed,
                   x, x_sb, x_again)
        node_phase(nc, sh, keep, x_sb, x_again, tables, out)


B_SECOND = 0
B_NODE = 2 * FEAT
B_END = B_NODE + FEAT

STEP = 7
X_PARTS = STEP
PIECES = 2 * STEP + 1


def run_turns(eng, turns, body, first=1):
    for turn in range(first):
        body(turn)
    with eng.Fori(first, turns - 1) as turn:
        body(turn)
    body(turns - 1)


def load_nodes(eng, sh, x, x_sb, loaded):
    J, full = sh.per_part, P - 1
    tail = sh.nodes - full * J
    width = J // len(loaded)
    for n, range_in in enumerate(loaded):
        j0, j1 = n * width, (n + 1) * width
        for a, b in ((0, 112), (112, full)):
            eng.dma_start(x_sb[a:b, j0:j1, :],
                          x[a * J:b * J, :].rearrange("(p j) f -> p j f", j=J)[:, j0:j1, :]).then_inc(range_in, 16)
        if n == 0:
            for at, rows in ((0, x[full * J:sh.nodes, :]), (tail, x[0:J - tail, :])):
                eng.dma_start(x_sb[full:P, at:at + rows.shape[0], :],
                              rows.rearrange("(p j) f -> p j f", p=1)).then_inc(range_in, 16)


def table_pieces(sh, tables):
    pieces = []
    for table in tables:
        runs = table[0:sh.slots, :].rearrange("(p c r) f -> p c (r f)", p=P, c=2 * STEP)
        pieces += [runs[:, c, :] for c in range(2 * STEP)]
        pieces.append(table[sh.slots:sh.slots + P, :])
    assert len(pieces) == PIECES * len(tables) and len(pieces) % CLEARING == 0
    assert EARLY % CLEARING == 0 and LATE % CLEARING == 0
    return pieces


def clear_tables(eng, zeros, pieces, cleared, first, end):
    for n in range(first, end):
        turn, r = divmod(n, len(cleared))
        if turn:
            eng.wait_ge(cleared[r], 16 * turn)
        eng.dma_start(pieces[n], zeros[:, 0:pieces[n].shape[1]]).then_inc(cleared[r], 16)


def prepare(nc, sh, keep, x, src, dst, Wo1, bo1, Wo2, bo2, Wi1, bi1, Wi2, bi2, Wn1, bn1, Wn2, bn2,
            proj, row_keys, bases, pieces, tables_zeroed):
    cols, ident, tri, pid, spare = (keep[k] for k in ("cols", "ident", "tri", "pid", "spare"))
    NB, J = sh.blocks, sh.per_part
    steps = J // STEP
    turns = steps // 2
    assert J % (2 * STEP) == 0
    whole = (sh.groups - 1) // P
    odd = sh.groups - 1 - whole * P
    halves = (slice(0, J // 2), slice(J // 2, J))
    FIRST = 4

    with ExitStack() as ctx:
        def sb(name, shape, dt=F32):
            return ctx.enter_context(nc.sbuf_tensor(name, shape, dt))

        def sem(name):
            return ctx.enter_context(nc.semaphore(name))

        src_i = sb("src_i", [P, NB, GROUP], I32)
        dst_i = sb("dst_i", [P, NB, GROUP], I32)
        slot_r = sb("slot_r", [P, NB, GROUP])
        out_r = sb("out_r", [P, NB, GROUP])
        key_r = src_i[:].bitcast(F32)
        rows_u = dst_i[:].bitcast(U16).rearrange("q b (k e) -> q b k e", k=2)
        dmin = sb("dmin", [P, NB])
        dmax = sb("dmax", [P, NB])
        base2 = sb("base2", [P, NB])
        base_i = sb("base_i", [P, NB], I32)
        wide = sb("wide", [P, NB])
        wide1 = sb("wide1", [P, 1])
        wide_all = sb("wide_all", [1, 1])
        w_node = sb("w_node", [P, 2 * HID])
        b_row = sb("b_row", [1, B_END])
        b_rest = sb("b_rest", [1, B_END])
        b_parts = sb("b_parts", [1, 3, B_END], BF16)
        eps = sb("eps", [P, 1])
        total = sb("total", [P, J])
        var = sb("var", [P, J])
        rstd = sb("rstd", [P, J])
        x_sb = sb("x_sb", [P, J, FEAT])
        squares1 = sb("squares1", [P, J // 2, FEAT])
        squares = (slot_r[:].rearrange("q b e -> q (b e)")[:, 0:J // 2 * FEAT].rearrange("p (j f) -> p j f", f=FEAT),
                   squares1[:])
        normed = sb("normed", [P, 2, STEP, FEAT])
        hT = sb("hT", [P, 2, STEP, P])
        proj_sb = sb("proj_sb", [P, 2, STEP, 2 * HID])

        ps_hT = ctx.enter_context(nc.psum_tensor("ps_hT", [P, 2 * 512], F32))
        ps_proj = ctx.enter_context(nc.psum_tensor("ps_proj", [P, 4 * 512], F32))

        weights_in = sem("weights_in")
        x_in = [sem(f"x_in{h}") for h in range(2)]
        src_in = sem("src_in")
        dst_in = sem("dst_in")
        const_made = sem("const_made")
        zero_made = sem("zero_made")
        chain = sem("chain")
        biases_split = sem("biases_split")
        biases_in = sem("biases_in")
        cleared = sem("cleared")
        centred = sem("centred")
        squared = sem("squared")
        var_made = sem("var_made")
        rooted = sem("rooted")
        rstd_made = sem("rstd_made")
        normed_made = sem("normed_made")
        hT_tr = sem("hT_tr")
        hT_made = sem("hT_made")
        proj_done = sem("proj_done")
        proj_copied = sem("proj_copied")
        proj_stored = [sem(f"proj_stored{r}") for r in range(2)]
        base_made = sem("base_made")
        rows_made = sem("rows_made")
        rows_stored = sem("rows_stored")
        padded = sem("padded")
        b_first_in = sem("b_first_in")
        bases_out = sem("bases_out")
        bases_in = sem("bases_in")
        fields_made = sem("fields_made")
        col_tr = sem("col_tr")
        slot_copied = sem("slot_copied")
        key_copied = sem("key_copied")
        masks_made = sem("masks_made")
        flag_tr = sem("flag_tr")

        block = ctx.enter_context(nc.Block())

        N_WEIGHTS = 12
        N_CONST = 6
        zeros = keep["zeros"]

        def block_groups(b):
            return slice(b * P, min((b + 1) * P, sh.groups))

        def column_psum(n):
            q = min(P, sh.groups - n // 2 * P)
            return ps_proj[:, 512 * (n % 4):512 * (n % 4) + 512].rearrange("p (t q) -> p q t", t=TILES)[:, 0:q, :]

        @block.sync
        def _(sp):
            load_nodes(sp, sh, x, x_sb, x_in)
            for ids, ids_i, ids_in in ((src, src_i, src_in), (dst, dst_i, dst_in)):
                sp.dma_start(ids_i[:, 0:whole, :],
                             ids[0:whole * P * GROUP].rearrange("(b q e) -> q b e", q=P, e=GROUP)).then_inc(ids_in, 16)
                for at, n, e0 in ((0, odd, whole * P * GROUP), (odd, 1, sh.last_e0), (odd + 1, P - odd - 1, 0)):
                    sp.dma_start(ids_i[at:at + n, whole, :],
                                 ids[e0:e0 + n * GROUP].rearrange("(q e) -> q e", e=GROUP)).then_inc(ids_in, 16)
            sp.wait_ge(zero_made, 1)
            clear_tables(sp, keep["zeros"], pieces, tables_zeroed, 0, EARLY)
            with nc.allow_non_contiguous_dma(reason="one base a group, once"):
                sp.wait_ge(base_made, 1)
                sp.dma_start(bases.rearrange("b q -> q b"), base_i[:]).then_inc(bases_out, 16)
            sp.wait_ge(rows_made, 1)
            sp.dma_start(row_keys.rearrange("(b q) k -> q b k", q=P),
                         rows_u.rearrange("q b k e -> q b (k e)")).then_inc(rows_stored, 16)
            sp.wait_ge(bases_out, 16)
            sp.dma_start(keep["base_row"][:], bases.rearrange("(a b) q -> a (b q)", a=1)).then_inc(bases_in, 16)
            sp.wait_ge(biases_split, 3)
            for k in range(3):
                sp.dma_start(keep["bias3"][k:k + 1, :], b_parts[:, k, :]).then_inc(biases_in, 16)
            clear_tables(sp, keep["zeros"], pieces, tables_zeroed, EARLY, len(pieces))
            sp.wait_ge(biases_in, 16 * 3)
            sp.wait_ge(rows_stored, 16)
            sp.wait_ge(bases_in, 16)

        @block.gpsimd
        def _(pool):
            pool.memset(ident[:], 0.0).then_inc(cleared, 1)
            pool.memset(tri[:], 1.0).then_inc(cleared, 1)
            pool.memset(keep["ones3"][:], 1.0).then_inc(const_made, 1)
            pool.memset(eps[:], EPS).then_inc(const_made, 1)
            pool.iota(pid[:], pattern=[[0, 1]], base=0, channel_multiplier=1,
                      allow_small_or_imprecise_dtypes=True).then_inc(const_made, 1)
            pool.iota(spare[:], pattern=[[0, 1]], base=sh.slots, channel_multiplier=1,
                      allow_small_or_imprecise_dtypes=True).then_inc(const_made, 1)
            pool.wait_ge(cleared, 2)
            pool.affine_select(out=ident[:], in_=ident[:], compare_op=ALU.not_equal, fill=1.0, base=0,
                               pattern=[[-1, P]], channel_multiplier=1).then_inc(const_made, 1)
            pool.affine_select(out=tri[:], in_=tri[:], compare_op=ALU.is_ge, fill=0.0, base=0,
                               pattern=[[1, P]], channel_multiplier=-1).then_inc(const_made, 1)
            pool.memset(zeros[:], 0.0).then_inc(zero_made, 1)
            pool.wait_ge(rstd_made, 1)

            def norm(turn):
                for r in range(2):
                    s = turn * 2 + r
                    if not isinstance(turn, int) or (s + 1) * STEP > J // 2:
                        pool.wait_ge(rstd_made, 2)
                    nodes = bass.ds(s * STEP, STEP)
                    if not isinstance(turn, int) or turn > 0:
                        pool.wait_ge(hT_tr, s - 1)
                    pool.tensor_tensor(normed[:, r, :, :], x_sb[:, nodes, :],
                                       rstd[:, nodes].unsqueeze(2).to_broadcast([P, STEP, FEAT]),
                                       ALU.mult).then_inc(normed_made, 1)
            run_turns(pool, turns, norm)
            for b in range(NB):
                pool.wait_ge(slot_copied, b + 1)
                groups = block_groups(b)
                pool.tensor_scalar(cols[:, groups, C_REL], cols[:, groups, C_SLOT], spare[:, 0:1], None, ALU.subtract)

        @block.scalar
        def _(act):
            for at, b in ((B_SECOND, bi2), (B_SECOND + FEAT, bo2), (B_NODE, bn2)):
                act.dma_start(b_row[:, at:at + b.shape[0]], b.rearrange("(a n) -> a n", a=1)).then_inc(weights_in, 16)
            for dst_ap, src_ap in (
                (w_node[0:FEAT, 0:HID], Wi1[0:FEAT, :]), (w_node[0:FEAT, HID:2 * HID], Wo1[0:FEAT, :]),
                (keep["w_edge"][0:FEAT, :], Wi1[FEAT:2 * FEAT, :]), (keep["w_edge"][FEAT:P, :], Wo1[FEAT:2 * FEAT, :]),
                (keep["w_second"][:, 0:FEAT], Wi2), (keep["w_second"][:, FEAT:2 * FEAT], Wo2),
                (keep["w_n1"][:], Wn1), (keep["w_n2"][:], Wn2),
                (keep["b_n1"][:], bn1.rearrange("(p a) -> p a", a=1)),
            ):
                act.dma_start(dst_ap, src_ap).then_inc(weights_in, 16)
            act.wait_ge(padded, 1)
            for at, b in ((0, bi1), (HID, bo1)):
                act.dma_start(w_node[FEAT:FEAT + 1, at:at + HID],
                              b.rearrange("(a n) -> a n", a=1)).then_inc(b_first_in, 16)
            act.wait_ge(const_made, N_CONST)
            for h, nodes in enumerate(halves):
                act.wait_ge(centred, h + 1)
                act.activation(squares[h], x_sb[:, nodes, :], ACT.Square).then_inc(squared, 1)
                act.wait_ge(var_made, h + 1)
                act.activation(rstd[:, nodes], var[:, nodes], ACT.Sqrt, scale=1.0 / FEAT,
                               bias=eps[:]).then_inc(rooted, 1)

            def relu_nodes(s, r):
                act.wait_ge(hT_tr, s + 1)
                if not isinstance(s, int) or s >= 2:
                    act.wait_ge(proj_done, 2 * s - 2)
                act.activation(hT[0:FEAT, r, :, :].rearrange("p t n -> p (t n)"), ps_hT[0:FEAT, 0:STEP * P],
                               ACT.Relu).then_inc(hT_made, 1)

            def step(s, r, turn):
                for part, tiles in enumerate((slice(0, FIRST), slice(FIRST, STEP))):
                    act.wait_ge(proj_done, 2 * s + part + 1)
                    if part == 0 and (not isinstance(s, int) or s >= 2):
                        act.wait_ge(proj_stored[r], turn * 16)
                    act.activation(proj_sb[:, r, tiles, :].rearrange("p t n -> p (t n)"),
                                   ps_proj[:, tiles.start * 2 * HID:tiles.stop * 2 * HID],
                                   ACT.Copy).then_inc(proj_copied, 1)
                act.wait_ge(proj_copied, 2 * s + 2)
                lot = STEP * 2 * HID
                act.dma_start(proj.rearrange("(p j) n -> p (j n)", j=J)[:, bass.ds(s * lot, lot)],
                              proj_sb[:, r, :, :].rearrange("p t n -> p (t n)")).then_inc(proj_stored[r], 16)

            def body(turn):
                for r in range(2):
                    s = turn * 2 + r
                    if not isinstance(s, int) or s + 1 < steps:
                        relu_nodes(s + 1, 1 - r)
                    step(s, r, turn)
            relu_nodes(0, 0)
            run_turns(act, turns, body)
            for b in range(NB):
                act.wait_ge(col_tr, 2 * b + 2)
                act.activation(cols[:, block_groups(b), C_KEY], column_psum(2 * b + 1),
                               ACT.Copy).then_inc(key_copied, 1)
            for r in range(2):
                act.wait_ge(proj_stored[r], 16 * turns)

        @block.vector
        def _(dve):
            links = [0]

            def link(ins):
                links[0] += 1
                ins.then_inc(chain, 1)
                dve.wait_ge(chain, links[0])

            nc.vector.memset(w_node[FEAT:P, :], 0.0).then_inc(padded, 1)
            link(nc.vector.memset(hT[FEAT:P, :, :, :], 0.0))
            nc.vector.memset(hT[FEAT:FEAT + 1, :, :, :], 1.0).then_inc(padded, 1)

            first, second = halves

            def centre(h, nodes):
                nc.vector.scalar_tensor_tensor(x_sb[:, nodes, :],
                                               total[:, nodes].unsqueeze(2).to_broadcast([P, J // 2, FEAT]),
                                               -1.0 / FEAT, x_sb[:, nodes, :], ALU.mult, ALU.add).then_inc(centred, 1)

            def sum_squares(h, nodes):
                dve.wait_ge(squared, h + 1)
                nc.vector.tensor_reduce(var[:, nodes], squares[h], AX_X, ALU.add).then_inc(var_made, 1)

            def invert(h, nodes):
                dve.wait_ge(rooted, h + 1)
                nc.vector.reciprocal(rstd[:, nodes], rstd[:, nodes]).then_inc(rstd_made, 1)

            dve.wait_ge(x_in[0], 16 * 4)
            link(nc.vector.tensor_reduce(total[:, first], x_sb[:, first, :], AX_X, ALU.add))
            centre(0, first)
            dve.wait_ge(x_in[1], 16 * 2)
            link(nc.vector.tensor_reduce(total[:, second], x_sb[:, second, :], AX_X, ALU.add))
            sum_squares(0, first)
            centre(1, second)
            invert(0, first)
            sum_squares(1, second)

            dve.wait_ge(src_in, 16 * 4)
            dve.wait_ge(dst_in, 16 * 4)
            link(nc.vector.tensor_tensor(out_r[:], src_i[:], dst_i[:], ALU.is_lt))
            invert(1, second)
            dve.wait_ge(var_made, 1)
            link(nc.vector.scalar_tensor_tensor(slot_r[:], src_i[:], 2.0, out_r[:], ALU.mult, ALU.add))
            link(nc.vector.scalar_tensor_tensor(key_r, dst_i[:], 2.0, out_r[:], ALU.mult, ALU.add))
            nc.vector.tensor_reduce(dmin[:], dst_i[:], AX_X, ALU.min)
            link(nc.vector.tensor_reduce(dmax[:], dst_i[:], AX_X, ALU.max))
            link(nc.vector.tensor_scalar(dmin[:], dmin[:], float(sh.padded - WINDOW), None, ALU.min))
            nc.vector.tensor_copy(base_i[:], dmin[:]).then_inc(base_made, 1)
            nc.vector.tensor_scalar(base2[:], dmin[:], 2.0, None, ALU.mult)
            link(nc.vector.tensor_tensor(wide[:], dmax[:], dmin[:], ALU.subtract))
            nc.vector.tensor_reduce(wide1[:], wide[:], AX_X, ALU.max).then_inc(fields_made, 1)
            for b in range(NB):
                nc.vector.tensor_copy(rows_u[:, b, 0, :].rearrange("q (t p) -> q p t", t=TILES),
                                      slot_r[:, b, :].rearrange("q (p t) -> q p t", t=TILES))
                last = nc.vector.tensor_scalar(rows_u[:, b, 1, :].rearrange("q (t p) -> q p t", t=TILES),
                                               key_r[:, b, :].rearrange("q (p t) -> q p t", t=TILES),
                                               base2[:, b:b + 1], None, ALU.subtract)
            last.then_inc(rows_made, 1)

            dve.wait_ge(weights_in, 16 * N_WEIGHTS)
            nc.vector.tensor_copy(b_parts[:, 0, :], b_row[:]).then_inc(biases_split, 1)
            dve.wait_ge(biases_split, 1)
            link(nc.vector.tensor_tensor(b_rest[:], b_row[:], b_parts[:, 0, :], ALU.subtract))
            nc.vector.tensor_copy(b_parts[:, 1, :], b_rest[:]).then_inc(biases_split, 1)
            dve.wait_ge(biases_split, 2)
            link(nc.vector.tensor_tensor(b_rest[:], b_rest[:], b_parts[:, 1, :], ALU.subtract))
            nc.vector.tensor_copy(b_parts[:, 2, :], b_rest[:]).then_inc(biases_split, 1)

            def masks(b):
                groups = block_groups(b)
                dve.wait_ge(slot_copied, b + 1)
                dve.wait_ge(key_copied, b + 1)
                for kind, op in ((C_IN, ALU.is_gt), (C_OUT, ALU.is_lt)):
                    nc.vector.tensor_tensor(cols[:, groups, kind], cols[:, groups, C_SLOT], cols[:, groups, C_KEY],
                                            op).then_inc(masks_made, 1)
            for b in range(NB):
                dve.wait_ge(col_tr, 2 * b + 1)
                nc.vector.tensor_copy(cols[:, block_groups(b), C_SLOT], column_psum(2 * b)).then_inc(slot_copied, 1)
                if b:
                    masks(b - 1)
            masks(NB - 1)
            dve.wait_ge(flag_tr, 1)
            link(nc.vector.tensor_reduce(wide_all[:], ps_hT[0:1, 0:P], AX_X, ALU.max))
            nc.vector.tensor_scalar(keep["flag"][:], wide_all[:], float(WINDOW - 1), None, ALU.is_gt)
            dve.wait_ge(masks_made, 2 * NB)
            nc.vector.memset(cols[0:sh.repeated // TILES, sh.groups - 1, C_MASKS], 0.0)

        @block.tensor
        def _(pe):
            held = pe.alloc_register("held")
            pe.wait_ge(const_made, N_CONST)
            pe.wait_ge(weights_in, 16 * N_WEIGHTS)
            pe.wait_ge(padded, 2)
            pe.wait_ge(b_first_in, 16 * 2)

            def turn_over(s, r):
                due, copied = s + 1, s
                if not isinstance(s, int):
                    pe.reg_mov(held, due)
                    pe.reg_mov(held, copied)
                pe.wait_ge(normed_made, 1)
                pe.wait_ge(normed_made, due)
                if not isinstance(s, int) or s >= 1:
                    pe.wait_ge(hT_made, copied)
                for t in range(STEP):
                    last = nc.tensor.transpose(ps_hT[0:FEAT, t * P:(t + 1) * P], normed[:, r, t, :], ident[:])
                last.then_inc(hT_tr, 1)

            def project(s, r):
                pe.wait_ge(hT_made, s + 1)
                for part, tiles in enumerate((range(0, FIRST), range(FIRST, STEP))):
                    if not isinstance(s, int) or s >= 1:
                        pe.wait_ge(proj_copied, 2 * s - 1 + part)
                    for t in tiles:
                        o = ps_proj[:, t * 2 * HID:(t + 1) * 2 * HID]
                        last = nc.tensor.matmul(o, hT[:, r, t, :], w_node[:], start=True, stop=True)
                    last.then_inc(proj_done, 1)

            def body(turn):
                for r in range(2):
                    s = turn * 2 + r
                    if not isinstance(s, int) or s + 1 < steps:
                        turn_over(s + 1, 1 - r)
                    project(s, r)
            turn_over(0, 0)
            run_turns(pe, turns, body)
            pe.wait_ge(fields_made, 1)
            nc.tensor.transpose(ps_hT[0:1, 0:P], wide1[:], ident[:]).then_inc(flag_tr, 1)
            pe.wait_ge(proj_copied, 2 * steps)
            for n in range(2 * NB):
                b, field = n // 2, (slot_r[:], key_r)[n % 2]
                if n >= 4:
                    pe.wait_ge((slot_copied, key_copied)[n % 2], b - 1)
                for t in range(TILES):
                    last = nc.tensor.transpose(ps_proj[:, 512 * (n % 4) + t * P:512 * (n % 4) + (t + 1) * P],
                                               field[:, b, :].rearrange("q (p t) -> q t p", t=TILES)[:, t, :],
                                               ident[:])
                last.then_inc(col_tr, 1)


class Group:

    def __init__(self, it, s):
        self.n = it * 4 + s
        self.ring4, self.ring2 = s % 4, s % 2
        self.turn = it + s // 4


def run_steps(eng, groups, lag, step):
    turns = groups // 4
    for i in range(8):
        step(0, i)
    with eng.Fori(2, turns) as it:
        for s in range(4):
            step(it, s)
    for s in range(groups + lag - 4 * turns):
        step(turns, s)


def edge_phase(nc, sh, keep, ea, proj, row_keys, tables, late_pieces, tables_zeroed, late_zeroed,
               x, x_sb, x_again):
    cols, ident, tri, pid, spare = (keep[k] for k in ("cols", "ident", "tri", "pid", "spare"))
    G = sh.groups
    LAG = 3

    with ExitStack() as ctx:
        def sb(name, shape, dt=F32):
            return ctx.enter_context(nc.sbuf_tensor(name, shape, dt))

        def ps(name, shape):
            return ctx.enter_context(nc.psum_tensor(name, shape, F32))

        def sem(name):
            return ctx.enter_context(nc.semaphore(name))

        edges_sb = sb("edges_sb", [P, 4, TILES, FEAT])
        keys_sb = sb("keys_sb", [P, 4, 2, GROUP], U16)
        window = sb("window", [P, 4, HID])
        col = sb("col", [P, 4, FIELDS])
        masked = sb("masked", [P, 2, TILES, 2, FEAT])
        onehot = sb("onehot", [P, 2, GROUP])
        same = sb("same", [P, 4, TILES, P])
        later = sb("later", [P, 4, TILES])
        kept = sb("kept", [P, 2, TILES])
        slot_u = sb("slot_u", [P, 4, TILES], U32)
        key_u = sb("key_u", [P, 2, TILES], U32)
        picked = sb("picked", [P, 2, TILES, HID])
        maskedT = sb("maskedT", [P, 2, GROUP])
        hidden = sb("hidden", [P, 2, GROUP])
        both = sb("both", [P, 2, TILES, 2, FEAT])
        message = sb("message", [P, 2, TILES, FEAT])
        flow_sb = sb("flow_sb", [P, 4, TILES, FEAT])

        ps_t = ps("ps_t", [P, 2, 512])
        ps_h = ps("ps_h", [P, 2, 512])
        ps_z = ps("ps_z", [P, 2, 512])
        ps_f = ps("ps_f", [P, 2, 512])

        edges_in = [sem(f"edges_in{r}") for r in range(4)]
        keys_in = [sem(f"keys_in{r}") for r in range(4)]
        window_in = [sem(f"window_in{r}") for r in range(4)]
        picked_in = [sem(f"picked_in{r}") for r in range(2)]
        added = [sem(f"added{t}") for t in range(TILES)]
        col_made = sem("col_made")
        masked_made = sem("masked_made")
        onehot_made = sem("onehot_made")
        key_made = sem("key_made")
        same_made = sem("same_made")
        kept_made = sem("kept_made")
        slot_made = sem("slot_made")
        both_made = sem("both_made")
        message_made = sem("message_made")
        transposed = sem("transposed")
        maskedT_made = sem("maskedT_made")
        first_done = sem("first_done")
        hidden_made = sem("hidden_made")
        second_done = sem("second_done")
        summed = sem("summed")
        flow_made = sem("flow_made")

        block = ctx.enter_context(nc.Block())

        def each_path(eng, program):
            with eng.register("wide_flag") as flag:
                eng.reg_load(flag, keep["flag"][0:1, 0:1])
                with eng.If_eq(flag, 0):
                    program(False)
                with eng.Else():
                    program(True)

        @block.sync
        def _(sp):
            def program(general):
                def load(it, s):
                    g = Group(it, s)
                    i = g.n
                    static = isinstance(i, int)
                    r = g.ring4
                    e0 = min(i * GROUP, sh.last_e0) if static else i * GROUP
                    if not static or i >= 4:
                        sp.wait_ge(masked_made, i - 3)
                    sp.dma_start(edges_sb[:, r, :, :].rearrange("p t f -> p (t f)"),
                                 ea[bass.ds(e0, GROUP), :].rearrange("(p t) f -> p (t f)", t=TILES)
                                 ).then_inc(edges_in[r], 16)
                    if not static or i >= 4:
                        sp.wait_ge(same_made, i - 3)
                        if not general:
                            sp.wait_ge(onehot_made, i - 3)
                    sp.dma_start(keys_sb[:, r, :, :].rearrange("p k e -> p (k e)"),
                                 row_keys[bass.ds(i, 1), :].to_broadcast([P, 2 * GROUP])).then_inc(keys_in[r], 16)
                    if not general:
                        base = sp.value_load(keep["base_row"][0:1, bass.ds(i, 1)], min_val=0,
                                             max_val=sh.padded - WINDOW)
                        if not static or i >= 4:
                            sp.wait_ge(first_done, i - 3)
                        sp.dma_start(window[:, r, :],
                                     proj[bass.ds(base, WINDOW), :].rearrange("n (d h) -> (n d) h", d=2)
                                     ).then_inc(window_in[r], 16)
                run_steps(sp, G, 0, load)
            each_path(sp, program)
            load_nodes(sp, sh, x, x_sb, [x_again] * X_PARTS)

        @block.vector
        def _(dve):
            def program(general):
                def step(it, s):
                    g, d = Group(it, s), Group(it, s - LAG)
                    i, j = g.n, d.n
                    static = isinstance(i, int)
                    front, back = not static or i < G, not static or 0 <= j < G
                    old = not static or i >= 4
                    r = g.ring4
                    if front:
                        if old:
                            dve.wait_ge(kept_made, i - 3)
                        nc.vector.tensor_copy(col[:, r, :],
                                              cols[:, bass.ds(i, 1), :].rearrange("p a k -> p (a k)")
                                              ).then_inc(col_made, 1)
                    if back:
                        dve.wait_ge(second_done, j + 1)
                        if not static or j >= 2:
                            dve.wait_ge(message_made, j - 1)
                        nc.vector.scalar_tensor_tensor(
                            both[:, d.ring2, :, :, :].rearrange("p t d f -> p (t d) f"),
                            ps_z[:, d.ring2, :].rearrange("p (m f) -> p m f", f=FEAT), 0.0,
                            col[:, d.ring4, C_MASKS].unsqueeze(2).to_broadcast([P, 2 * TILES, FEAT]),
                            ALU.max, ALU.mult).then_inc(both_made, 1)
                    if front:
                        dve.wait_ge(col_made, i + 1)
                        dve.wait_ge(edges_in[r], 16 * (g.turn + 1))
                        if old or i >= 2:
                            dve.wait_ge(transposed, i - 1)
                        nc.vector.tensor_tensor(
                            masked[:, g.ring2, :, :, :],
                            edges_sb[:, r, :, :].unsqueeze(2).to_broadcast([P, TILES, 2, FEAT]),
                            col[:, r, C_MASKS].rearrange("p (t d) -> p t d", d=2).unsqueeze(3)
                            .to_broadcast([P, TILES, 2, FEAT]), ALU.mult).then_inc(masked_made, 1)
                        dve.wait_ge(keys_in[r], 16 * (g.turn + 1))
                        if old:
                            dve.wait_ge(summed, i - 3)
                        for t in range(TILES):
                            last = nc.vector.scalar_tensor_tensor(
                                same[:, r, t, :], keys_sb[:, r, 0, t * P:(t + 1) * P], col[:, r, t:t + 1],
                                tri[:], ALU.is_equal, ALU.mult, accum_out=later[:, r, t:t + 1])
                        last.then_inc(same_made, 1)
                    if back:
                        dve.wait_ge(both_made, j + 1)
                        if not static or j >= 2:
                            dve.wait_ge(summed, j - 1)
                        nc.vector.tensor_tensor(message[:, d.ring2, :, :], both[:, d.ring2, :, 0, :],
                                                both[:, d.ring2, :, 1, :], ALU.add).then_inc(message_made, 1)
                        dve.wait_ge(same_made, j + 1)
                        if not static or j >= 2:
                            dve.wait_ge(slot_made, j - 1)
                        nc.vector.scalar_tensor_tensor(
                            kept[:, d.ring2, :], later[:, d.ring4, :], 1.0, col[:, d.ring4, C_REL],
                            ALU.is_equal, ALU.mult).then_inc(kept_made, 1)
                    if front:
                        if general:
                            if not static or i >= 2:
                                rounds = i // 2 if static else it * 2 + s // 2
                                dve.wait_ge(picked_in[g.ring2], 16 * TILES * rounds)
                            nc.vector.tensor_copy(key_u[:, g.ring2, :], col[:, r, C_KEY]).then_inc(key_made, 1)
                        else:
                            if not static or i >= 2:
                                dve.wait_ge(first_done, i - 1)
                            nc.vector.tensor_scalar(onehot[:, g.ring2, :], keys_sb[:, r, 1, :], pid[:, 0:1], None,
                                                    ALU.is_equal).then_inc(onehot_made, 1)
                    if back:
                        dve.wait_ge(kept_made, j + 1)
                        if not static or j >= 4:
                            for t in range(TILES):
                                dve.wait_ge(added[t], 16 * (j - 3))
                        nc.vector.tensor_scalar(slot_u[:, d.ring4, :], kept[:, d.ring2, :], spare[:, 0:1], None,
                                                ALU.add).then_inc(slot_made, 1)
                run_steps(dve, G, LAG, step)
            each_path(dve, program)

        @block.tensor
        def _(pe):
            def program(general):
                def step(it, s):
                    a, b, c, d = (Group(it, s - k) for k in range(4))
                    static = isinstance(a.n, int)

                    def on(g):
                        return not static or 0 <= g.n < G
                    if on(a):
                        pe.wait_ge(masked_made, a.n + 1)
                        if not static or a.n >= 2:
                            pe.wait_ge(maskedT_made, a.n - 1)
                        for t in range(TILES):
                            last = nc.tensor.transpose(
                                ps_t[:, a.ring2, t * P:(t + 1) * P],
                                masked[:, a.ring2, t, :, :].rearrange("p d f -> p (d f)"), ident[:])
                        last.then_inc(transposed, 1)
                    if on(c):
                        pe.wait_ge(hidden_made, c.n + 1)
                        if not static or c.n >= 2:
                            pe.wait_ge(both_made, c.n - 1)
                        nc.tensor.matmul(
                            ps_z[:, c.ring2, :].rearrange("p (t n) -> p t n", t=TILES), keep["ones3"][:],
                            keep["bias3"][:, B_SECOND:B_SECOND + 2 * FEAT].unsqueeze(1).to_broadcast([3, TILES, 2 * FEAT]),
                            start=True, stop=False)
                        for t in range(TILES):
                            last = nc.tensor.matmul(
                                ps_z[:, c.ring2, t * P:(t + 1) * P], hidden[:, c.ring2, t * P:(t + 1) * P],
                                keep["w_second"][:], start=False, stop=(t == TILES - 1))
                        last.then_inc(second_done, 1)
                    if on(b):
                        pe.wait_ge(maskedT_made, b.n + 1)
                        if not static or b.n >= 2:
                            pe.wait_ge(hidden_made, b.n - 1)
                        nc.tensor.matmul(ps_h[:, b.ring2, :], keep["w_edge"][:], maskedT[:, b.ring2, :],
                                         start=True, stop=False)
                        if general:
                            rounds = b.n // 2 if static else it * 2 + (s - 1) // 2
                            pe.wait_ge(picked_in[b.ring2], 16 * TILES * (rounds + 1))
                            for t in range(TILES):
                                last = nc.tensor.matmul(ps_h[:, b.ring2, t * P:(t + 1) * P],
                                                        picked[:, b.ring2, t, :], ident[:],
                                                        start=False, stop=(t == TILES - 1))
                        else:
                            pe.wait_ge(window_in[b.ring4], 16 * (b.turn + 1))
                            pe.wait_ge(onehot_made, b.n + 1)
                            last = nc.tensor.matmul(ps_h[:, b.ring2, :], window[:, b.ring4, :],
                                                    onehot[:, b.ring2, :], start=False, stop=True)
                        last.then_inc(first_done, 1)
                    if on(d):
                        pe.wait_ge(message_made, d.n + 1)
                        pe.wait_ge(same_made, d.n + 1)
                        if not static or d.n >= 2:
                            pe.wait_ge(flow_made, d.n - 1)
                        for t in range(TILES):
                            last = nc.tensor.matmul(ps_f[:, d.ring2, t * FEAT:(t + 1) * FEAT], same[:, d.ring4, t, :],
                                                    message[:, d.ring2, t, :], start=True, stop=True)
                        last.then_inc(summed, 1)
                run_steps(pe, G, LAG, step)
            each_path(pe, program)

        @block.scalar
        def _(act):
            def program(general):
                def step(it, s):
                    a, b, d = Group(it, s), Group(it, s - 1), Group(it, s - 3)
                    static = isinstance(a.n, int)

                    def on(g):
                        return not static or 0 <= g.n < G
                    if on(a):
                        act.wait_ge(transposed, a.n + 1)
                        if not static or a.n >= 2:
                            act.wait_ge(first_done, a.n - 1)
                        act.activation(maskedT[:, a.ring2, :], ps_t[:, a.ring2, :], ACT.Copy).then_inc(maskedT_made, 1)
                    if on(b):
                        act.wait_ge(first_done, b.n + 1)
                        if not static or b.n >= 2:
                            act.wait_ge(second_done, b.n - 1)
                        act.activation(hidden[:, b.ring2, :], ps_h[:, b.ring2, :], ACT.Relu).then_inc(hidden_made, 1)
                    if on(d):
                        act.wait_ge(summed, d.n + 1)
                        if not static or d.n >= 4:
                            for t in range(TILES):
                                act.wait_ge(added[t], 16 * (d.n - 3))
                        act.activation(flow_sb[:, d.ring4, :, :].rearrange("p t f -> p (t f)"),
                                       ps_f[:, d.ring2, 0:TILES * FEAT], ACT.Copy).then_inc(flow_made, 1)
                run_steps(act, G, LAG, step)
            each_path(act, program)

        @block.gpsimd
        def _(pool):
            held = pool.alloc_register("held")

            def value(v):
                if not isinstance(v, int):
                    pool.reg_mov(held, v)
                return v

            def program(general):
                def step(it, s):
                    g, d = Group(it, s), Group(it, s - LAG)
                    static = isinstance(g.n, int)
                    if general and (not static or g.n < G):
                        keys_due, free_due = value(g.n + 1), value(g.n - 1)
                        pool.wait_ge(key_made, 1)
                        pool.wait_ge(key_made, keys_due)
                        if not static or g.n >= 2:
                            pool.wait_ge(first_done, free_due)
                        for t in range(TILES):
                            pool.indirect_dma_start(
                                out=picked[:, g.ring2, t, :], out_offset=None,
                                in_=proj.rearrange("n (d h) -> (n d) h", d=2),
                                in_offset=bass.IndirectOffsetOnAxis(ap=key_u[:, g.ring2, t:t + 1], axis=0),
                            ).then_inc(picked_in[g.ring2], 16)
                    if not static or 0 <= d.n < G:
                        due, added_due = value(d.n + 1), value(16 * d.n)
                        pool.wait_ge(flow_made, 1)
                        pool.wait_ge(flow_made, due)
                        pool.wait_ge(slot_made, due)
                        for t in range(TILES):
                            if not static or d.n >= 1:
                                if t:
                                    pool.wait_ge(flow_made, 1)
                                pool.wait_ge(added[t], added_due)
                            pool.indirect_dma_start(
                                out=tables[t],
                                out_offset=bass.IndirectOffsetOnAxis(ap=slot_u[:, d.ring4, t:t + 1], axis=0),
                                in_=flow_sb[:, d.ring4, t, :], in_offset=None, compute_op=ALU.add,
                            ).then_inc(added[t], 16)
                run_steps(pool, G, LAG, step)
            clear_tables(pool, keep["zeros"], late_pieces, late_zeroed, 0, LATE)
            early_turns = (len(tables) * PIECES - LATE) // CLEARING
            for zeroed in tables_zeroed:
                pool.wait_ge(zeroed, 16 * early_turns)
            for zeroed in late_zeroed:
                pool.wait_ge(zeroed, 16 * LATE // CLEARING)
            each_path(pool, program)
            for t in range(TILES):
                pool.wait_ge(added[t], 16 * G)


def node_phase(nc, sh, keep, x_sb, x_again, tables, out):
    ident = keep["ident"]
    J = sh.per_part
    steps = J // STEP
    RING = 4
    LOT = STEP * 2 * FEAT
    full = P - 1
    tail = sh.nodes - full * J
    pieces = [(0, steps - RING), (steps - RING, steps - 1), (steps - 1, steps)]

    with ExitStack() as ctx:
        def sb(name, shape, dt=F32):
            return ctx.enter_context(nc.sbuf_tensor(name, shape, dt))

        def ps(name, shape):
            return ctx.enter_context(nc.psum_tensor(name, shape, F32))

        def sem(name):
            return ctx.enter_context(nc.semaphore(name))

        parts = sb("parts", [P, RING, TILES, LOT])
        pairs = sb("pairs", [P, 2, 2, LOT])
        flow = sb("flow", [P, 2, STEP, 2 * FEAT])
        flowT = sb("flowT", [P, 2, STEP * P])
        hid = sb("hid", [P, 2, STEP * P])
        outs = x_sb

        ps_flow = ps("ps_flow", [P, 2 * 512])
        ps_hid = ps("ps_hid", [P, 2 * 512])
        ps_out = ps("ps_out", [P, 2, 512])

        parts_in = [sem(f"parts_in{r}") for r in range(RING)]
        front_made = sem("front_made")
        back_made = sem("back_made")
        flow_added = sem("flow_added")
        flow_tr = sem("flow_tr")
        flowT_made = sem("flowT_made")
        hid_done = sem("hid_done")
        hid_made = sem("hid_made")
        out_done = sem("out_done")
        out_made = sem("out_made")
        out_stored = sem("out_stored")

        block = ctx.enter_context(nc.Block())
        flat = [t[0:sh.slots, :].rearrange("(p j) f -> p (j f)", p=P) for t in tables]

        def run_steps_of_four(eng, lag, step):
            turns = steps // 4
            for k in range(4):
                step(0, k)
            with eng.Fori(1, turns) as turn:
                for k in range(4):
                    step(turn, k)
            for k in range(steps + lag - 4 * turns):
                step(turns, k)

        @block.sync
        def _(sp):
            def load(turn, k):
                s, r = turn * 4 + k, k % RING
                if not isinstance(s, int) or s >= RING:
                    sp.wait_ge(front_made, s - RING + 1)
                    sp.wait_ge(back_made, s - RING + 1)
                for t in range(TILES):
                    sp.dma_start(parts[:, r, t, :], flat[t][:, bass.ds(s * LOT, LOT)]).then_inc(parts_in[r], 16)
            run_steps_of_four(sp, 0, load)

            sent = 0
            whole = out[0:full * J, :].rearrange("(p j) f -> p j f", j=J)
            for first, end in pieces:
                a, b = first * STEP, end * STEP
                sp.wait_ge(out_made, end)
                for p0, p1 in ((0, 112), (112, full)):
                    sp.dma_start(whole[p0:p1, a:b, :], outs[p0:p1, a:b, :]).then_inc(out_stored, 16)
                    sent += 1
                if a < tail:
                    b = min(b, tail)
                    sp.dma_start(out[full * J + a:full * J + b, :].rearrange("(p j) f -> p j f", p=1),
                                 outs[full:P, a:b, :]).then_inc(out_stored, 16)
                    sent += 1
            sp.wait_ge(out_stored, 16 * sent)

        @block.gpsimd
        def _(pool):
            def back(turn, k):
                s, r, r4 = turn * 4 + k, k % 2, k % RING
                pool.wait_ge(parts_in[r4], (turn + 1) * (16 * TILES))
                if not isinstance(s, int) or s >= 2:
                    pool.wait_ge(flow_added, s - 1)
                pool.tensor_tensor(pairs[:, r, 1, :], parts[:, r4, 2, :], parts[:, r4, 3, :],
                                   ALU.add).then_inc(back_made, 1)
            run_steps_of_four(pool, 0, back)

        @block.vector
        def _(dve):
            dve.wait_ge(x_again, 16 * (2 * X_PARTS + 2))

            def step(turn, k):
                s, r, r4 = turn * 4 + k, k % 2, k % RING
                static = isinstance(s, int)
                if not static or s < steps:
                    dve.wait_ge(parts_in[r4], (turn + 1) * (16 * TILES))
                    if not static or s >= 2:
                        dve.wait_ge(flow_added, s - 1)
                    nc.vector.tensor_tensor(pairs[:, r, 0, :], parts[:, r4, 0, :], parts[:, r4, 1, :],
                                            ALU.add).then_inc(front_made, 1)
                    dve.wait_ge(front_made, s + 1)
                    dve.wait_ge(back_made, s + 1)
                    if not static or s >= 2:
                        dve.wait_ge(flow_tr, s - 1)
                    nc.vector.tensor_tensor(flow[:, r, :, :].rearrange("p t n -> p (t n)"), pairs[:, r, 0, :],
                                            pairs[:, r, 1, :], ALU.add).then_inc(flow_added, 1)
                if not static or s >= 3:
                    j = s - 3
                    dve.wait_ge(out_done, s - 2)
                    nc.vector.scalar_tensor_tensor(
                        outs[:, bass.ds(j * STEP, STEP), :],
                        ps_out[:, 1 - r, 0:STEP * FEAT].rearrange("p (t f) -> p t f", f=FEAT),
                        0.0, x_sb[:, bass.ds(j * STEP, STEP), :], ALU.max, ALU.add).then_inc(out_made, 1)
            run_steps_of_four(dve, 3, step)

        @block.tensor
        def _(pe):
            def step(turn, k):
                s, r = turn * 4 + k, k % 2
                static = isinstance(s, int)
                if not static or s < steps:
                    pe.wait_ge(flow_added, s + 1)
                    if not static or s >= 1:
                        pe.wait_ge(flowT_made, s)
                    for t in range(STEP):
                        last = nc.tensor.transpose(ps_flow[:, t * P:(t + 1) * P], flow[:, r, t, :], ident[:])
                    last.then_inc(flow_tr, 1)
                if not static or 1 <= s <= steps:
                    pe.wait_ge(flowT_made, s)
                    if not static or s >= 2:
                        pe.wait_ge(hid_made, s - 1)
                    for a, b in ((0, 512), (512, STEP * P)):
                        last = nc.tensor.matmul(ps_hid[:, a:b], keep["w_n1"][:], flowT[:, 1 - r, a:b],
                                                start=True, stop=True)
                    last.then_inc(hid_done, 1)
                if not static or s >= 2:
                    pe.wait_ge(hid_made, s - 1)
                    if not static or s >= 4:
                        pe.wait_ge(out_made, s - 3)
                    nc.tensor.matmul(ps_out[:, r, 0:STEP * FEAT].rearrange("p (t n) -> p t n", t=STEP),
                                     keep["ones3"][:],
                                     keep["bias3"][:, B_NODE:B_NODE + FEAT].unsqueeze(1).to_broadcast([3, STEP, FEAT]),
                                     start=True, stop=False)
                    for t in range(STEP):
                        last = nc.tensor.matmul(ps_out[:, r, t * FEAT:(t + 1) * FEAT], hid[:, r, t * P:(t + 1) * P],
                                                keep["w_n2"][:], start=False, stop=(t == STEP - 1))
                    last.then_inc(out_done, 1)
            run_steps_of_four(pe, 2, step)

        @block.scalar
        def _(act):
            def step(turn, k):
                s, r = turn * 4 + k, k % 2
                static = isinstance(s, int)
                if not static or s < steps:
                    act.wait_ge(flow_tr, s + 1)
                    if not static or s >= 2:
                        act.wait_ge(hid_done, s - 1)
                    act.activation(flowT[:, r, :], ps_flow[:, 0:STEP * P], ACT.Copy).then_inc(flowT_made, 1)
                if not static or 1 <= s <= steps:
                    act.wait_ge(hid_done, s)
                    if not static or s >= 3:
                        act.wait_ge(out_done, s - 2)
                    act.activation(hid[:, 1 - r, :], ps_hid[:, 0:STEP * P], ACT.Relu,
                                   bias=keep["b_n1"][:]).then_inc(hid_made, 1)
            run_steps_of_four(act, 1, step)


_INS = ['x', 'src', 'dst', 'edge_attr_64', 'L0_gnn_Wo1', 'L0_gnn_bo1', 'L0_gnn_Wo2', 'L0_gnn_bo2', 'L0_gnn_Wi1',
        'L0_gnn_bi1', 'L0_gnn_Wi2', 'L0_gnn_bi2', 'L0_gnn_Wn1', 'L0_gnn_bn1', 'L0_gnn_Wn2', 'L0_gnn_bn2']


def kernel(**inputs):
    import numpy as _np
    import concourse.bacc as _bacc
    from concourse import mybir as _mybir
    from concourse.bass_utils import run_bass_kernel_spmd as _run

    nc = _bacc.Bacc("TRN2", target_bir_lowering=False, num_devices=1)
    arrays, args = {}, []
    for name in _INS:
        a = _np.ascontiguousarray(inputs[name])
        arrays[f"in_{name}"] = a
        args.append(nc.dram_tensor(f"in_{name}", a.shape, _mybir.dt.from_np(a.dtype), kind="ExternalInput").ap())
    shape = inputs["x"].shape
    args.append(nc.dram_tensor("out", shape, _mybir.dt.float32, kind="ExternalOutput").ap())
    gnn_kernel(nc, *args)
    r = _run(nc, [arrays], core_ids=[0])
    return r.results[0]["out"]
```
